# Optimizing a Trainium2 kernel written in Bass

```python
import numpy as np
import jax
import jax.numpy as jnp

def _softmax(x, axis=-1):
    return jax.nn.softmax(x, axis=axis)

def _gelu(x):
    return jax.nn.gelu(x, approximate=True)

def _silu(x):
    return jax.nn.silu(x)

def _sigmoid(x):
    return jax.nn.sigmoid(x)

def _layernorm(x, axis=-1, eps=1e-05):
    m = jnp.mean(x, axis=axis, keepdims=True)
    v = jnp.var(x, axis=axis, keepdims=True)
    return (x - m) / jnp.sqrt(v + eps)

def _scatter_add(tgt, idx, src, axis=0):
    return tgt.at[idx].add(src)

def _segment_sum(src, seg, n):
    return jax.ops.segment_sum(src, seg, n)
kernel_name = 'mk_perceiver_d1_seqx_r2_d7e19f'

def setup_inputs(seed: int=0):
    np.random.seed(seed)
    _w = jnp.asarray

    def _rec_inputs():
        import jax
        import jax.numpy as jnp
        _rk = jax.random.key(seed)
        x = -7.109e-05 + 0.9999 * jax.random.normal(jax.random.fold_in(_rk, 1), (64, 32, 2048), jnp.float32)
        _lenS = 32 - jax.random.randint(jax.random.fold_in(_rk, 7), (64,), 0, max(1, 32 // 4) + 1, jnp.int32)
        _lenS2 = 257 - jax.random.randint(jax.random.fold_in(_rk, 8), (64,), 0, max(1, 257 // 4) + 1, jnp.int32)
        _ctx_4096P = jax.random.normal(jax.random.fold_in(_rk, 11), (64, 16, 2048), jnp.float32)
        _ctx_4096c = jax.random.dirichlet(jax.random.fold_in(_rk, 511), 0.3 * jnp.ones((16,), jnp.float32), (64, 257))
        _ctx_4096t = jnp.einsum('bsk,bkd->bsd', _ctx_4096c, _ctx_4096P)
        _ctx_4096t = _ctx_4096t * jax.lax.rsqrt(jnp.mean(jnp.square(_ctx_4096t)) + 1e-12) * 0.953939
        ctx_4096 = -0.00010331 + 0.999899 * (_ctx_4096t + 0.3 * jax.random.normal(jax.random.fold_in(_rk, 611), (64, 257, 2048), jnp.float32))
        return (x, ctx_4096)
    x, ctx_4096 = _rec_inputs()

    def _L0_xattn_setup():
        import jax, jax.numpy as jnp
        import numpy as np
        key = jax.random.key(seed)
        k1, k2 = jax.random.split(key)
        B, Lq, Lk, D = (16, 512, 1024, 2048)
        query = jax.random.normal(k1, (B, Lq, D), dtype=jnp.float32)
        key_t = jax.random.normal(k2, (B, Lk, D), dtype=jnp.float32)
        return {'query': query, 'key': key_t}
    _L0_xattn_all = _L0_xattn_setup()
    _L0_xattn_in = {k: v for k, v in _L0_xattn_all.items() if k in ()}
    del _L0_xattn_all

    def _L0_attn_setup():
        import jax, jax.numpy as jnp
        import numpy as np
        EMB_DIM = 2048
        N_HEADS = 32
        QKV_DIM = EMB_DIM // N_HEADS
        B, S = (4, 2048)
        key = jax.random.key(seed)
        ks = jax.random.split(key, 7)
        std = 1.0 / np.sqrt(EMB_DIM)
        x = jax.random.normal(ks[0], (B, S, EMB_DIM), dtype=jnp.float32)
        Wq = jax.random.normal(ks[1], (EMB_DIM, QKV_DIM, N_HEADS), dtype=jnp.float32) * std
        bq = jnp.zeros((QKV_DIM, N_HEADS), dtype=jnp.float32)
        Wk = jax.random.normal(ks[2], (EMB_DIM, QKV_DIM, 1), dtype=jnp.float32) * std
        bk = jnp.zeros((QKV_DIM, 1), dtype=jnp.float32)
        Wv = jax.random.normal(ks[3], (EMB_DIM, QKV_DIM, 1), dtype=jnp.float32) * std
        bv = jnp.zeros((QKV_DIM, 1), dtype=jnp.float32)
        return {'x': x, 'Wq': Wq, 'bq': bq, 'Wk': Wk, 'bk': bk, 'Wv': Wv, 'bv': bv}
    _L0_attn_all = _L0_attn_setup()
    _L0_attn_in = {k: v for k, v in _L0_attn_all.items() if k in ('Wq', 'bq', 'Wk', 'bk', 'Wv', 'bv')}
    del _L0_attn_all

    def _L0_ffn_setup():
        import jax, jax.numpy as jnp
        import numpy as np
        OUT, IN, GROUP = (2048, 2048, 32)
        NGROUPS = OUT * IN // GROUP
        key = jax.random.key(seed)
        k1, k2, k3, k4 = jax.random.split(key, 4)
        x = jax.random.normal(k1, (4, 1024, IN), dtype=jnp.float32)
        weight_q3 = jax.random.randint(k2, (NGROUPS, GROUP), 0, 8, dtype=jnp.int32)
        ranges = jnp.sort(jax.random.normal(k3, (NGROUPS, 2), dtype=jnp.float32), axis=-1)
        weight_ranges = ranges.astype(jnp.float16)
        bias = jax.random.normal(k4, (OUT,), dtype=jnp.float16)
        return {'x': x, 'weight_q3': weight_q3, 'weight_ranges': weight_ranges, 'bias': bias}
    _L0_ffn_all = _L0_ffn_setup()
    _L0_ffn_in = {k: v for k, v in _L0_ffn_all.items() if k in ('weight_q3', 'weight_ranges', 'bias')}
    del _L0_ffn_all
    return {'x': x, 'ctx_4096': ctx_4096, 'L0_attn_Wq': _L0_attn_in['Wq'], 'L0_attn_bq': _L0_attn_in['bq'], 'L0_attn_Wk': _L0_attn_in['Wk'], 'L0_attn_bk': _L0_attn_in['bk'], 'L0_attn_Wv': _L0_attn_in['Wv'], 'L0_attn_bv': _L0_attn_in['bv'], 'L0_ffn_weight_q3': _L0_ffn_in['weight_q3'], 'L0_ffn_weight_ranges': _L0_ffn_in['weight_ranges'], 'L0_ffn_bias': _L0_ffn_in['bias']}

def reference(x, ctx_4096, L0_attn_Wq, L0_attn_bq, L0_attn_Wk, L0_attn_bk, L0_attn_Wv, L0_attn_bv, L0_ffn_weight_q3, L0_ffn_weight_ranges, L0_ffn_bias):
    import jax
    import jax.numpy as jnp

    def _L0_xattn_ref(query, key):
        import jax, jax.numpy as jnp
        import numpy as np
        a = jnp.einsum('bqd,bkd->bqk', query, key)
        e = jax.nn.softmax(a, axis=-1)
        c = jnp.einsum('bqk,bkd->bqd', e, key)
        return c

    def _L0_attn_ref(x, Wq, bq, Wk, bk, Wv, bv):
        import jax, jax.numpy as jnp
        import numpy as np
        EMB_DIM = 2048
        N_HEADS = 32
        QKV_DIM = EMB_DIM // N_HEADS
        B, S = (4, 2048)
        q = jnp.einsum('bsD,Ddh->bsdh', x, Wq) + bq
        k = (jnp.einsum('bsD,Ddh->bsdh', x, Wk) + bk)[..., 0]
        v = (jnp.einsum('bsD,Ddh->bsdh', x, Wv) + bv)[..., 0]
        qkv_dim = q.shape[-2]
        n_heads = q.shape[-1]
        scale = 1.0 / jnp.sqrt(jnp.asarray(qkv_dim, dtype=q.dtype))
        scores = jnp.einsum('bsdh,bse->bsde', q, k) * scale
        p = jax.nn.softmax(scores, axis=-1)
        o = jnp.einsum('bsde,bse->bsd', p, v)
        out = jnp.broadcast_to(o[..., None], o.shape + (n_heads,))
        return out.reshape(x.shape[:-1] + (qkv_dim * n_heads,))

    def _L0_ffn_ref(x, weight_q3, weight_ranges, bias):
        import jax, jax.numpy as jnp
        import numpy as np
        OUT, IN, GROUP = (2048, 2048, 32)
        NGROUPS = OUT * IN // GROUP
        r = weight_ranges.astype(jnp.float32)
        x_min = r[:, 0:1]
        x_max = r[:, 1:2]
        w = weight_q3.astype(jnp.float32) / 7.0 * (x_max - x_min) + x_min
        w = w.reshape(OUT, IN)
        out = jnp.einsum('bsi,oi->bso', x, w) + bias.astype(jnp.float32)
        return out
    x = x + _L0_xattn_ref(_layernorm(x, axis=-1), ctx_4096)
    x = x + _L0_attn_ref(_layernorm(x, axis=-1), L0_attn_Wq, L0_attn_bq, L0_attn_Wk, L0_attn_bk, L0_attn_Wv, L0_attn_bv)
    x = x + _L0_ffn_ref(_layernorm(x, axis=-1), L0_ffn_weight_q3, L0_ffn_weight_ranges, L0_ffn_bias)
    return x

_drawn_inputs = setup_inputs


def setup_inputs(seed=0):
    import zlib

    import numpy as np

    out = dict(_drawn_inputs(seed))
    spreads = {'L0_attn_bq': (0.0, 0.1), 'L0_attn_bk': (0.0, 0.1), 'L0_attn_bv': (0.0, 0.1)}
    factors = {}
    for name, (base, spread) in spreads.items():
        noise = np.random.default_rng([zlib.crc32(name.encode()), seed]).standard_normal(out[name].shape)
        drawn = base * np.exp(spread * noise) if base else spread * noise
        out[name] = jnp.asarray(drawn.astype(out[name].dtype))
    for name, factor in factors.items():
        out[name] = (out[name] * factor).astype(out[name].dtype)
    return out
```

```python
from contextlib import ExitStack

import concourse.bass as bass
from concourse import mybir

F32 = mybir.dt.float32
F16 = mybir.dt.float16
BF16 = mybir.dt.bfloat16
I32 = mybir.dt.int32
ALU = mybir.AluOpType
ACT = mybir.ActivationFunctionType
AX = mybir.AxisListType

P = 128
EPS = 1e-5
LO = 2048.0


def wait(eng, sem, value):
    if isinstance(value, int) and value <= 0:
        return
    eng.wait_ge(sem, value)


def pass_by(eng, passed):
    eng.sem_inc(passed, 1)


def at(eng, value):
    return value if isinstance(value, int) else eng.snap(value)


def chain(eng, sem, base):
    state = [0]

    def link(instruction):
        state[0] += 1
        instruction.then_inc(sem, 1)
        eng.wait_ge(sem, base + state[0])

    return link


def build(nc, x, ctx_kv, Wq, bq, Wk, bk, Wv, bv, q3, ranges, bias, out):
    B, Q, D = x.shape
    K = ctx_kv.shape[1]
    DH, H = Wq.shape[1], Wq.shape[2]
    NB = P // Q
    NT = B // NB
    DC = D // P
    KC = K // P
    DB = D // 512
    CPB = 512 // P
    NW = 3 * DH
    GROUP = q3.shape[1]
    G = D // GROUP
    assert K == KC * P + 1 and D == DH * H and NT % 2 == 0

    x_tok = x.rearrange("b q d -> (b q) d")
    out_tok = out.rearrange("b q d -> (b q) d")
    x2_dram = nc.dram_tensor("x2_scratch", (B * Q, D), F32).ap()

    with ExitStack() as ctx:
        def sb(name, shape, dt):
            return ctx.enter_context(nc.sbuf_tensor(name, shape, dt))

        def sem(name):
            return ctx.enter_context(nc.semaphore(name))

        ident = sb("ident", [P, P], F32)
        consts = sb("consts", [P, len(NORM_CONSTS)], F32)
        consts_ready = sem("consts_ready")

        attention(nc, ident, consts, consts_ready, x_tok, ctx_kv, Wq, bq, Wk, bk, Wv, bv, x2_dram,
                  NT, NB, Q, D, DC, KC, DB, CPB, DH, H, NW)
        feed_forward(nc, ident, consts, x2_dram, q3, ranges, bias, out_tok, NT, D, DC, DB, CPB, GROUP, G)


def norm_factors(nc, pool, link, stats, factors, consts):
    v, y, a, r, nb = (factors[:, n:n + 1] for n in range(5))
    minus_half, eps, three_halves, minus_one = (consts[:, n:n + 1] for n in range(4))
    link(nc.gpsimd.tensor_tensor(v, stats[:, 1:2], eps, ALU.add))
    link(nc.gpsimd.tensor_tensor(y, v, minus_half, ALU.pow))
    link(nc.gpsimd.tensor_tensor(a, y, y, ALU.mult))
    link(nc.gpsimd.tensor_tensor(a, a, v, ALU.mult))
    link(nc.gpsimd.tensor_tensor(a, a, minus_half, ALU.mult))
    link(nc.gpsimd.tensor_tensor(a, a, three_halves, ALU.add))
    link(nc.gpsimd.tensor_tensor(r, y, a, ALU.mult))
    link(nc.gpsimd.tensor_tensor(a, stats[:, 0:1], r, ALU.mult))
    return nc.gpsimd.tensor_tensor(nb, a, minus_one, ALU.mult)


NORM_LINKS = 8
NORM_CONSTS = (-0.5, EPS, 1.5, -1.0)
CONSTS_READY = 6


def attention(nc, ident, consts, consts_ready, x_tok, ctx_kv, Wq, bq, Wk, bk, Wv, bv, x2_dram,
              NT, NB, Q, D, DC, KC, DB, CPB, DH, H, NW):
    SCALE = float(DH) ** -0.5
    NS = 4
    DS = DH // NS
    K0 = KC * P
    WRING = 2
    with ExitStack() as ctx:
        def sb(name, shape, dt=F32):
            return ctx.enter_context(nc.sbuf_tensor(name, shape, dt))

        def psum(name, shape):
            return ctx.enter_context(nc.psum_tensor(name, shape, F32))

        def sem(name):
            return ctx.enter_context(nc.semaphore(name))

        keys = sb("keys", [P, DB, NB, KC, 512])
        last = sb("last", [P, D])
        xa = sb("xa", [P, 2, D])
        xb = sb("xb", [P, 2, D])
        xn1 = sb("xn1", [P, D])
        xn2 = sb("xn2", [P, D])
        xn1T = sb("xn1T", [P, DC, P])
        xn2T = sb("xn2T", [P, DC, P])
        keysT = sb("keysT", [P, 4, NB, K0])
        wqkv = sb("wqkv", [P, DC, NW])
        wstage = sb("wstage", [P, WRING, DH * H])
        bias_qkv = sb("bias_qkv", [P, NW])
        prod = sb("prod", [P, 2, DS, DH])
        junk = sb("junk", [P, D], BF16)
        probs = sb("probs", [P, K0])
        probsT = sb("probsT", [P, KC, P])
        qkv = sb("qkv", [P, NW])
        bn1 = sb("bn1", [P, DB, 6])
        bn2 = sb("bn2", [P, DB, 6])
        mv1 = sb("mv1", [P, 2])
        mv2 = sb("mv2", [P, 2])
        nf1 = sb("nf1", [P, 5])
        nf2 = sb("nf2", [P, 5])
        s_last = sb("s_last", [P, 1])
        row = sb("row", [P, 8])
        kext = sb("kext", [P, 2])
        qlow = sb("qlow", [P, DH])
        top = sb("top", [P, DH])
        den = sb("den", [P, DH])
        num = sb("num", [P, DH])
        rden = sb("rden", [P, DH])
        o = sb("o", [P, DH])

        bank = [psum(f"bank{n}", [P, 512]) for n in range(4)]
        scores = psum("scores", [P, 512])
        pvb = [psum(f"pv{n}", [P, 512]) for n in range(2)]
        mixed = psum("mixed", [P, 512])

        x_loaded = [sem(f"x_loaded{n}") for n in range(2)]
        last_loaded = sem("last_loaded")
        keys_loaded = [sem(f"keys_loaded{n}") for n in range(DB)]
        w_loaded = [sem(f"w_loaded{n}") for n in range(WRING)]
        small_loaded = sem("small_loaded")
        wkv_loaded = sem("wkv_loaded")
        w_summed = sem("w_summed")
        bank_full = [sem(f"bank_full{n}") for n in range(4)]
        bank_emptied = [sem(f"bank_emptied{n}") for n in range(4)]
        chunk_scored = sem("chunk_scored")
        qkv_done = sem("qkv_done")
        qkv_read = sem("qkv_read")
        probsT_done = sem("probsT_done")
        probsT_read = sem("probsT_read")
        pv_filled = sem("pv_filled")
        pv_emptied = sem("pv_emptied")
        stats1_ready = sem("stats1_ready")
        stats2_ready = sem("stats2_ready")
        factors1_ready = sem("factors1_ready")
        factors2_ready = sem("factors2_ready")
        xn1_ready = sem("xn1_ready")
        xn2_ready = sem("xn2_ready")
        last_scored = sem("last_scored")
        negmax_ready = sem("negmax_ready")
        probs_ready = sem("probs_ready")
        residual_ready = sem("residual_ready")
        top_ready = sem("top_ready")
        prod_ready = sem("prod_ready")
        exp_ready = sem("exp_ready")
        den_ready = sem("den_ready")
        weighted_ready = sem("weighted_ready")
        num_ready = sem("num_ready")
        o_ready = sem("o_ready")
        x2_ready = sem("x2_ready")
        x2_stored = [sem(f"x2_stored{n}") for n in range(2)]
        softmax_step = sem("softmax_step")
        dve_passed = sem("dve_passed")
        sp_passed = sem("sp_passed")
        top_step = sem("top_step")
        ext_step = sem("ext_step")
        bn1_step = sem("bn1_step")
        bn2_step = sem("bn2_step")
        rden_step = sem("rden_step")
        bias_step = sem("bias_step")
        outer_step = sem("outer_step")
        norm1_step = sem("norm1_step")
        norm2_step = sem("norm2_step")

        def use(i, k):
            return i * 10 + (k - 1)

        def tiles(eng, tile):
            tile(0, 0)
            tile(1, 1)
            with eng.Fori(1, NT // 2 - 1) as j:
                tile(j * 2, 0)
                tile(j * 2 + 1, 1)
            tile(NT - 2, 0)
            tile(NT - 1, 1)

        def landed(i, p):
            return i * 8 + (16 - 8 * p)

        block = ctx.enter_context(nc.Block())

        @block.sync
        def _(sp):
            def load_x(i, p):
                row0 = at(sp, i * P)
                wait(sp, residual_ready, i - 1)
                sp.dma_start(xa[:, p, :], x_tok[bass.ds(row0, P), :]).then_inc(x_loaded[p], 16)

            def load_context(i):
                batch = [at(sp, i * NB + b) for b in range(NB)]
                wait(sp, residual_ready, i)
                for b in range(NB):
                    sp.dma_start(last[b * Q:(b + 1) * Q, :],
                                 ctx_kv[bass.ds(batch[b], 1), K0, :].broadcast_to((Q, D))
                                 ).then_inc(last_loaded, 16)
                for d in range(DB):
                    wait(sp, pv_filled, i * DB + (d + 1 - DB))
                    pass_by(sp, sp_passed)
                    for b in range(NB):
                        sp.dma_start(keys[:, d, b],
                                     ctx_kv[bass.ds(batch[b], 1), 0:K0, d * 512:(d + 1) * 512]
                                     .rearrange("a (c p) n -> p (a c) n", p=P)
                                     ).then_inc(keys_loaded[d], 16)

            def store_x2(i, p):
                row0 = at(sp, i * P)
                wait(sp, x2_ready, i + 1)
                sp.dma_start(x2_dram[bass.ds(row0, P), :], xb[:, p, :]).then_inc(x2_stored[p], 16)

            load_x(0, 0)
            load_context(0)

            def tile(i, p):
                if not isinstance(i, int) or i + 1 < NT:
                    load_x(i + 1, 1 - p)
                    load_context(i + 1)
                if not isinstance(i, int) or i > 0:
                    store_x2(i - 1, 1 - p)

            tiles(sp, tile)
            store_x2(NT - 1, 1)
            for p in range(2):
                sp.wait_ge(x2_stored[p], 16 * (NT // 2))

        @block.tensor
        def _(pe):
            def turn(i, k, s, blocks, ready=None):
                wait(pe, bank_emptied[s], use(i, k) - 1)
                for j, block_in in enumerate(blocks):
                    mm = nc.tensor.transpose(bank[s][:, j * P:(j + 1) * P], block_in, ident[:])
                mm.then_inc(bank_full[s], 1)

            def turn_tokens(i, k, source):
                for u in range(4):
                    turn(i, k, u, [source[:, (4 * u + j) * P:(4 * u + j + 1) * P] for j in range(4)])

            def turn_chunk(i, c):
                if c % CPB == 0:
                    pe.wait_ge(keys_loaded[c // CPB], (i + 1) * (16 * NB))
                for h in range(2):
                    turn(i, 3 + c // 2, 2 * (c % 2) + h,
                         [keys[:, c // CPB, 2 * h + b, kc, (c % CPB) * P:(c % CPB + 1) * P]
                          for b in range(2) for kc in range(KC)])

            def score_chunk(i, c):
                if c == 0:
                    wait(pe, probs_ready, i * 2)
                if c % 4 == 0:
                    pe.wait_ge(bank_emptied[c // 4], use(i, 2))
                for h in range(2):
                    pe.wait_ge(bank_emptied[2 * (c % 2) + h], use(i, 3 + c // 2))
                for b in range(NB):
                    mm = nc.tensor.matmul(scores[b * Q:(b + 1) * Q, 0:K0], xn1T[:, c, b * Q:(b + 1) * Q],
                                          keysT[:, c % 4, b, :], start=(c == 0), stop=(c == DC - 1))
                mm.then_inc(chunk_scored, 1)

            def project(i):
                wait(pe, probsT_read, i)
                for u in range(4):
                    pe.wait_ge(bank_emptied[u], use(i, 1))
                pe.wait_ge(w_summed, DC)
                pe.wait_ge(wkv_loaded, 32)
                for c in range(DC):
                    mm = nc.tensor.matmul(mixed[:, 0:NW], xn2T[:, c, :], wqkv[:, c, :],
                                          start=(c == 0), stop=(c == DC - 1))
                mm.then_inc(qkv_done, 1)

            def tile(i, p):
                if not isinstance(i, int) or i > 0:
                    pe.wait_ge(xn2_ready, i)
                    turn_tokens(i, 1, xn2)
                pe.wait_ge(xn1_ready, i + 1)
                turn_tokens(i, 2, xn1)
                turn_chunk(i, 0)
                if not isinstance(i, int) or i > 0:
                    project(i)
                for c in range(DC):
                    if c + 1 < DC:
                        turn_chunk(i, c + 1)
                    score_chunk(i, c)
                wait(pe, qkv_read, i)
                pe.wait_ge(probs_ready, (i + 1) * 2)
                for kc in range(KC):
                    mm = nc.tensor.transpose(mixed[:, kc * P:(kc + 1) * P], probs[:, kc * P:(kc + 1) * P],
                                             ident[:])
                mm.then_inc(probsT_done, 1)
                pe.wait_ge(probsT_read, i + 1)
                for d in range(DB):
                    wait(pe, pv_emptied, i * DB + (d - 1))
                    for kc in range(KC):
                        for b in range(NB):
                            mm = nc.tensor.matmul(pvb[d % 2][b * Q:(b + 1) * Q, :],
                                                  probsT[:, kc, b * Q:(b + 1) * Q], keys[:, d, b, kc, :],
                                                  start=(kc == 0), stop=(kc == KC - 1))
                    mm.then_inc(pv_filled, 1)

            pe.wait_ge(consts_ready, CONSTS_READY)
            tiles(pe, tile)
            pe.wait_ge(xn2_ready, NT)
            turn_tokens(NT, 1, xn2)
            project(NT)

        @block.scalar
        def _(act):
            def empty(i, k, s, target):
                act.wait_ge(bank_full[s], use(i, k))
                nc.scalar.copy(target, bank[s][:]).then_inc(bank_emptied[s], 1)

            def exp_slice(i, s):
                n = i * NS + (s + 1 - NS)
                act.wait_ge(prod_ready, n)
                nc.scalar.activation(prod[:, s % 2], prod[:, s % 2], ACT.Exp, scale=SCALE).then_inc(exp_ready, 1)

            def chunk(i, c):
                wait(act, chunk_scored, i * DC + (c - 3))
                for h in range(2):
                    s = 2 * (c % 2) + h
                    if s < 3:
                        empty(i, 3 + c // 2, s, keysT[:, c % 4, 2 * h:2 * h + 2, :].rearrange("p b k -> p (b k)"))

            def normalise(count, factors_ready, xn_ready, target, source, factors):
                act.wait_ge(factors_ready, count)
                nc.scalar.activation(target, source, ACT.Identity, bias=factors[:, 4:5],
                                     scale=factors[:, 3:4]).then_inc(xn_ready, 1)

            def tile(i, p):
                later = not isinstance(i, int) or i > 0
                if later:
                    for u in range(3):
                        empty(i, 1, u, xn2T[:, 4 * u:4 * u + 4, :].rearrange("p c n -> p (c n)"))
                for u in range(3):
                    empty(i, 2, u, xn1T[:, 4 * u:4 * u + 4, :].rearrange("p c n -> p (c n)"))
                for c in range(DC):
                    chunk(i, c)
                    if c in (7, 11, 15) and later:
                        exp_slice(i, (c - 7) // 4)
                    if c == 9 and (not isinstance(i, int) or i + 1 < NT):
                        act.wait_ge(last_scored, i + 1)
                        act.wait_ge(bank_full[3], use(i, 2))
                        normalise(i + 2, factors1_ready, xn1_ready, xn1[:], xa[:, 1 - p, :], nf1)
                act.wait_ge(negmax_ready, i + 1)
                wait(act, probsT_done, i)
                nc.scalar.activation(probs[:], scores[:, 0:K0], ACT.Exp, bias=row[:, 1:2],
                                     accum_out=row[:, 2:3]).then_inc(probs_ready, 1)
                nc.scalar.activation(row[:, 3:4], s_last[:], ACT.Exp, bias=row[:, 1:2]).then_inc(probs_ready, 1)
                act.wait_ge(probsT_done, i + 1)
                nc.scalar.copy(probsT[:].rearrange("p c n -> p (c n)"), mixed[:, 0:K0]).then_inc(probsT_read, 1)
                if later:
                    act.wait_ge(bank_full[3], use(i, 1))
                normalise(i + 1, factors2_ready, xn2_ready, xn2[:], xb[:, p, :], nf2)
                if later:
                    exp_slice(i, 3)

            normalise(1, factors1_ready, xn1_ready, xn1[:], xa[:, 0, :], nf1)
            tiles(act, tile)
            for u in range(3):
                empty(NT, 1, u, xn2T[:, 4 * u:4 * u + 4, :].rearrange("p c n -> p (c n)"))
            for s in range(NS):
                exp_slice(NT, s)

        @block.vector
        def _(dve):
            def empty3(i, k, target):
                dve.wait_ge(bank_full[3], use(i, k))
                nc.vector.tensor_copy(target, bank[3][:]).then_inc(bank_emptied[3], 1)

            def stats1(i, p):
                dve.wait_ge(x_loaded[p], landed(i, p))
                wait(dve, factors1_ready, i)
                for d in range(DB):
                    nc.vector.bn_stats(bn1[:, d], xa[:, p, d * 512:(d + 1) * 512]).then_inc(bn1_step, 1)
                dve.wait_ge(bn1_step, (i + 1) * DB)
                pass_by(dve, dve_passed)
                nc.vector.bn_aggr(mv1[:], bn1[:].rearrange("p d s -> p (d s)")).then_inc(stats1_ready, 1)

            def qkv_out(i):
                dve.wait_ge(qkv_done, i)
                wait(dve, x2_ready, i - 1)
                nc.vector.tensor_tensor(qkv[:], mixed[:, 0:NW], bias_qkv[:], ALU.add).then_inc(qkv_read, 1)
                dve.wait_ge(qkv_read, i)
                nc.vector.tensor_reduce(kext[:, 0:1], qkv[:, DH:2 * DH], AX.X, ALU.max).then_inc(ext_step, 1)
                nc.vector.tensor_reduce(kext[:, 1:2], qkv[:, DH:2 * DH], AX.X, ALU.min).then_inc(ext_step, 1)
                dve.wait_ge(ext_step, i * 2)
                nc.vector.tensor_scalar(qlow[:], qkv[:, 0:DH], kext[:, 1:2], None, ALU.mult).then_inc(top_step, 1)
                dve.wait_ge(top_step, i)
                nc.vector.scalar_tensor_tensor(top[:], qkv[:, 0:DH], kext[:, 0:1], qlow[:],
                                               ALU.mult, ALU.max).then_inc(top_ready, 1)

            def reduce_slice(i, s):
                n = i * NS + (s + 1 - NS)
                dve.wait_ge(exp_ready, n)
                nc.vector.tensor_reduce(den[:, s * DS:(s + 1) * DS], prod[:, s % 2], AX.X,
                                        ALU.add).then_inc(den_ready, 1)
                dve.wait_ge(weighted_ready, n)
                nc.vector.tensor_reduce(num[:, s * DS:(s + 1) * DS], prod[:, s % 2], AX.X,
                                        ALU.add).then_inc(num_ready, 1)

            def finish_self(i):
                dve.wait_ge(den_ready, i * NS)
                nc.vector.reciprocal(rden[:], den[:]).then_inc(rden_step, 1)
                dve.wait_ge(rden_step, i)
                dve.wait_ge(num_ready, i * NS)
                nc.vector.tensor_tensor(o[:], num[:], rden[:], ALU.mult).then_inc(o_ready, 1)

            def sum_heads(c):
                dve.wait_ge(w_loaded[c % WRING], 16 * (c // WRING + 1))
                nc.vector.tensor_reduce(wqkv[:, c, 0:DH],
                                        wstage[:, c % WRING].rearrange("p (d h) -> p d h", h=H),
                                        AX.X, ALU.add).then_inc(w_summed, 1)

            def tile(i, p):
                later = not isinstance(i, int) or i > 0
                link = chain(dve, softmax_step, i * 4)
                if later:
                    empty3(i, 1, xn2T[:, 12:16, :].rearrange("p c n -> p (c n)"))
                empty3(i, 2, xn1T[:, 12:16, :].rearrange("p c n -> p (c n)"))
                for c in range(DC):
                    if c % 2:
                        wait(dve, chunk_scored, i * DC + (c - 3))
                        empty3(i, 3 + c // 2, keysT[:, c % 4, 2:4, :].rearrange("p b k -> p (b k)"))
                    if c == 1 and later:
                        qkv_out(i)
                    if c == 3:
                        dve.wait_ge(last_loaded, (i + 1) * (16 * NB))
                        wait(dve, probs_ready, i * 2)
                        nc.vector.tensor_tensor_reduce(out=junk[:], in0=xn1[:], in1=last[:], scale=1.0,
                                                       scalar=0.0, op0=ALU.mult, op1=ALU.add,
                                                       accum_out=s_last[:]).then_inc(last_scored, 1)
                    if c == 5 and (not isinstance(i, int) or i + 1 < NT):
                        stats1(i + 1, 1 - p)
                    if c in (7, 11, 15) and later:
                        reduce_slice(i, (c - 7) // 4)
                    if not later and c < DC // 2:
                        sum_heads(2 * c)
                        sum_heads(2 * c + 1)
                dve.wait_ge(chunk_scored, (i + 1) * DC)
                wait(dve, probs_ready, i * 2)
                link(nc.vector.tensor_reduce(row[:, 0:1], scores[:, 0:K0], AX.X, ALU.max))
                dve.wait_ge(last_scored, i + 1)
                nc.vector.tensor_scalar(row[:, 1:2], row[:, 0:1], s_last[:], -1.0, ALU.max,
                                        ALU.mult).then_inc(negmax_ready, 1)
                dve.wait_ge(probs_ready, (i + 1) * 2)
                link(nc.vector.tensor_tensor(row[:, 4:5], row[:, 2:3], row[:, 3:4], ALU.add))
                link(nc.vector.reciprocal(row[:, 5:6], row[:, 4:5]))
                link(nc.vector.tensor_tensor(row[:, 6:7], row[:, 3:4], row[:, 5:6], ALU.mult))
                if not isinstance(i, int) or i >= 2:
                    dve.wait_ge(x2_stored[p], landed(i, p) - 16)
                nc.vector.scalar_tensor_tensor(xb[:, p, :], last[:], row[:, 6:7], xa[:, p, :], ALU.mult,
                                               ALU.add).then_inc(residual_ready, 1)
                dve.wait_ge(residual_ready, i + 1)
                wait(dve, factors2_ready, i)
                for d in range(DB):
                    part = xb[:, p, d * 512:(d + 1) * 512]
                    dve.wait_ge(pv_filled, i * DB + (d + 1))
                    nc.vector.scalar_tensor_tensor(part, pvb[d % 2][:], row[:, 5:6], part, ALU.mult,
                                                   ALU.add).then_inc(pv_emptied, 1)
                    dve.wait_ge(pv_emptied, i * DB + (d + 1))
                    nc.vector.bn_stats(bn2[:, d], part).then_inc(bn2_step, 1)
                dve.wait_ge(bn2_step, (i + 1) * DB)
                pass_by(dve, dve_passed)
                nc.vector.bn_aggr(mv2[:], bn2[:].rearrange("p d s -> p (d s)")).then_inc(stats2_ready, 1)
                if later:
                    reduce_slice(i, 3)
                    finish_self(i)

            stats1(0, 0)
            dve.wait_ge(small_loaded, 48)
            nc.vector.tensor_reduce(bias_qkv[:, 0:DH], xn2[:].rearrange("p (d h) -> p d h", h=H), AX.X,
                                    ALU.add).then_inc(bias_step, 1)
            dve.wait_ge(bias_step, 1)
            tiles(dve, tile)
            empty3(NT, 1, xn2T[:, 12:16, :].rearrange("p c n -> p (c n)"))
            qkv_out(NT)
            for s in range(NS):
                reduce_slice(NT, s)
            finish_self(NT)

        @block.gpsimd
        def _(pool):
            def factors(i, step, mv, nf, stats_ready, factors_ready, xn_ready):
                link = chain(pool, step, i * NORM_LINKS)
                pool.wait_ge(stats_ready, i + 1)
                wait(pool, xn_ready, i)
                norm_factors(nc, pool, link, mv, nf, consts).then_inc(factors_ready, 1)

            def product(i, s):
                n = i * NS + (s + 1 - NS)
                wait(pool, num_ready, n - 2)
                S = prod[:, s % 2]
                nc.gpsimd.tensor_tensor(S, qkv[:, s * DS:(s + 1) * DS].unsqueeze(2).broadcast_to((P, DS, DH)),
                                        qkv[:, DH:2 * DH].unsqueeze(1).broadcast_to((P, DS, DH)),
                                        ALU.mult).then_inc(outer_step, 1)
                pool.wait_ge(outer_step, n)
                nc.gpsimd.tensor_tensor(S, S, top[:, s * DS:(s + 1) * DS].unsqueeze(2).broadcast_to((P, DS, DH)),
                                        ALU.subtract).then_inc(prod_ready, 1)

            def weigh(i, s):
                n = i * NS + (s + 1 - NS)
                pool.wait_ge(exp_ready, n)
                pool.wait_ge(den_ready, n)
                S = prod[:, s % 2]
                nc.gpsimd.tensor_tensor(S, S, qkv[:, 2 * DH:3 * DH].unsqueeze(1).broadcast_to((P, DS, DH)),
                                        ALU.mult).then_inc(weighted_ready, 1)

            def add_self(i, p):
                pool.wait_ge(o_ready, i)
                y = xb[:, p, :].rearrange("p (d h) -> p d h", h=H)
                nc.gpsimd.tensor_tensor(y, y, o[:].unsqueeze(2).broadcast_to((P, DH, H)),
                                        ALU.add).then_inc(x2_ready, 1)

            def tile(i, p):
                later = not isinstance(i, int) or i > 0
                if later:
                    pool.wait_ge(top_ready, i)
                    product(i, 0)
                    product(i, 1)
                if not isinstance(i, int) or i + 1 < NT:
                    factors(i + 1, norm1_step, mv1, nf1, stats1_ready, factors1_ready, xn1_ready)
                if later:
                    weigh(i, 0)
                    product(i, 2)
                    weigh(i, 1)
                    product(i, 3)
                    weigh(i, 2)
                factors(i, norm2_step, mv2, nf2, stats2_ready, factors2_ready, xn2_ready)
                if later:
                    weigh(i, 3)
                    pool.wait_ge(xn2_ready, i)
                    add_self(i, 1 - p)

            nc.gpsimd.memset(ident[:], 0.0).then_inc(consts_ready, 1)
            for n, value in enumerate(NORM_CONSTS):
                nc.gpsimd.memset(consts[:, n:n + 1], value).then_inc(consts_ready, 1)
            pool.wait_ge(consts_ready, CONSTS_READY - 1)
            nc.gpsimd.affine_select(out=ident[:], in_=ident[:], compare_op=ALU.not_equal, fill=1.0, base=0,
                                    pattern=[[-1, P]], channel_multiplier=1).then_inc(consts_ready, 1)
            pool.dma_start(xn2[:], bq.rearrange("d h -> (d h)").unsqueeze(0).broadcast_to((P, DH * H))
                           ).then_inc(small_loaded, 16)
            pool.dma_start(bias_qkv[:, DH:2 * DH], bk.rearrange("d o -> o d").broadcast_to((P, DH))
                           ).then_inc(small_loaded, 16)
            pool.dma_start(bias_qkv[:, 2 * DH:3 * DH], bv.rearrange("d o -> o d").broadcast_to((P, DH))
                           ).then_inc(small_loaded, 16)
            pool.dma_start(wqkv[:, :, DH:2 * DH], Wk.rearrange("(c p) d o -> p c (d o)", p=P)
                           ).then_inc(wkv_loaded, 16)
            pool.dma_start(wqkv[:, :, 2 * DH:3 * DH], Wv.rearrange("(c p) d o -> p c (d o)", p=P)
                           ).then_inc(wkv_loaded, 16)

            def load_w(c):
                wait(pool, w_summed, c - WRING + 1)
                pool.dma_start(wstage[:, c % WRING], Wq[c * P:(c + 1) * P].rearrange("p d h -> p (d h)")
                               ).then_inc(w_loaded[c % WRING], 16)

            for c in range(WRING):
                load_w(c)
            factors(0, norm1_step, mv1, nf1, stats1_ready, factors1_ready, xn1_ready)
            for c in range(WRING, DC):
                load_w(c)
            tiles(pool, tile)
            pool.wait_ge(top_ready, NT)
            product(NT, 0)
            product(NT, 1)
            for s in range(NS):
                weigh(NT, s)
                if s + 2 < NS:
                    product(NT, s + 2)
            pool.wait_ge(xn2_ready, NT)
            add_self(NT, 1)


def feed_forward(nc, ident, consts, x2_dram, q3, ranges, bias, out_tok, NT, D, DC, DB, CPB, GROUP, G):
    LEVELS = 7.0
    OT = D // P
    with ExitStack() as ctx:
        def sb(name, shape, dt=F32):
            return ctx.enter_context(nc.sbuf_tensor(name, shape, dt))

        def sem(name):
            return ctx.enter_context(nc.semaphore(name))

        w_high = sb("w_high", [P, DC, D], F16)
        w_low = sb("w_low", [P, DC, D], F16)
        rng = sb("rng", [P, OT, G, 2], F16)
        bias_row = sb("bias_row", [P, D], F16)
        w_nat = sb("w_nat", [P, 2, D])
        x2 = sb("x2", [P, 2, D])
        xn3 = sb("xn3", [P, D])
        step_of = xn3[:, 0:OT * G].rearrange("p (t g) -> p t g", g=G)
        least_of = xn3[:, OT * G:2 * OT * G].rearrange("p (t g) -> p t g", g=G)
        x_high = sb("x_high", [P, 2, DC, P], F16)
        x_low = sb("x_low", [P, 2, DC, P], F16)
        x_small = sb("x_small", [P, 2, DC, P], F16)
        bn3 = sb("bn3", [P, DB, 6])
        mv3 = sb("mv3", [P, 2])
        nf3 = sb("nf3", [P, 5])
        bank = [ctx.enter_context(nc.psum_tensor(f"turned{n}", [P, 512], F32)) for n in range(4)]
        y = [ctx.enter_context(nc.psum_tensor(f"y{n}", [P, 512], F32)) for n in range(DB)]

        rng_loaded = sem("rng_loaded")
        bias_loaded = sem("bias_loaded")
        w_loaded = [sem(f"rows_loaded{n}") for n in range(2)]
        x2_loaded = [sem(f"x2_loaded{n}") for n in range(2)]
        out_stored = [sem(f"out_stored{n}") for n in range(2)]
        range_step = sem("range_step")
        ranges_ready = sem("ranges_ready")
        scaled = sem("scaled")
        w_ready = sem("w_ready")
        turned_full = [sem(f"turned_full{n}") for n in range(4)]
        high_ready = sem("high_ready")
        turned_emptied = [sem(f"turned_emptied{n}") for n in range(4)]
        small_ready = sem("small_ready")
        bn3_step = sem("bn3_step")
        dve_passed3 = sem("dve_passed3")
        stats3_ready = sem("stats3_ready")
        norm3_step = sem("norm3_step")
        factors3_ready = sem("factors3_ready")
        xn3_ready = sem("xn3_ready")
        biased = sem("biased")
        y_filled = sem("y_filled")
        y_emptied = sem("y_emptied")

        def tiles(eng, tile):
            tile(0, 0)
            tile(1, 1)
            with eng.Fori(1, NT // 2 - 1) as j:
                tile(j * 2, 0)
                tile(j * 2 + 1, 1)
            tile(NT - 2, 0)
            tile(NT - 1, 1)

        def more(i):
            return not isinstance(i, int) or i + 1 < NT

        def landed(i, p):
            return i * 8 + (16 - 8 * p)

        block = ctx.enter_context(nc.Block())

        @block.sync
        def _(sp):
            q_rows = q3.rearrange("(t p g) r -> t p (g r)", p=P, g=G)

            def load_x2(i, p, freed=None):
                row0 = at(sp, i * P)
                if freed is not None:
                    sp.wait_ge(*freed)
                sp.dma_start(x2[:, p, :], x2_dram[bass.ds(row0, P), :]).then_inc(x2_loaded[p], 16)

            def store(i, p):
                row0 = at(sp, i * P)
                sp.wait_ge(y_emptied, i * DB + DB)
                sp.dma_start(out_tok[bass.ds(row0, P), :], x2[:, p, :]).then_inc(out_stored[p], 16)

            sp.dma_start(rng[:].rearrange("p t g r -> p t (g r)"),
                         ranges.rearrange("(t p g) r -> p t (g r)", p=P, g=G)).then_inc(rng_loaded, 16)
            for t in range(OT):
                wait(sp, turned_full[3], t - 1)
                sp.dma_start(w_nat[:, t % 2, :].bitcast(I32), q_rows[t]).then_inc(w_loaded[t % 2], 16)
                if t == 2:
                    load_x2(0, 0)
                    sp.dma_start(bias_row[:], bias.unsqueeze(0).broadcast_to((P, D))).then_inc(bias_loaded, 16)

            def tile(i, p):
                if isinstance(i, int) and i == 0:
                    load_x2(1, 1)
                    return
                store(i - 1, 1 - p)
                if more(i):
                    load_x2(i + 1, 1 - p, freed=(out_stored[1 - p], landed(i - 1, 1 - p)))

            tiles(sp, tile)
            store(NT - 1, 1)
            for p in range(2):
                sp.wait_ge(out_stored[p], 16 * (NT // 2))

        @block.tensor
        def _(pe):
            def turn(n, s, blocks):
                wait(pe, turned_emptied[s], n - 1)
                for j, block_in in enumerate(blocks):
                    mm = nc.tensor.transpose(bank[s][:, j * P:(j + 1) * P], block_in, ident[:])
                mm.then_inc(turned_full[s], 1)

            def turn_tokens(i):
                pe.wait_ge(xn3_ready, i + 1)
                for u in range(4):
                    turn(i + (OT + 1), u, [xn3[:, (4 * u + j) * P:(4 * u + j + 1) * P] for j in range(4)])

            def product(i, p, d):
                wait(pe, y_emptied, i * DB + (d + 1 - DB))
                cols = slice(d * 512, (d + 1) * 512)
                for c in range(DC):
                    nc.tensor.matmul(y[d][:], x_high[:, p, c, :], w_high[:, c, cols], start=(c == 0), stop=False)
                    nc.tensor.matmul(y[d][:], x_low[:, p, c, :], w_high[:, c, cols], start=False, stop=False)
                    mm = nc.tensor.matmul(y[d][:], x_small[:, p, c, :], w_low[:, c, cols], start=False,
                                          stop=(c == DC - 1))
                mm.then_inc(y_filled, 1)

            def tile(i, p):
                pe.wait_ge(small_ready, i + 1)
                product(i, p, 0)
                product(i, p, 1)
                if more(i):
                    turn_tokens(i + 1)
                product(i, p, 2)
                product(i, p, 3)

            for t in range(OT):
                pe.wait_ge(w_ready, t + 1)
                for u in range(4):
                    turn(t + 1, u, [w_nat[:, t % 2, (4 * u + j) * P:(4 * u + j + 1) * P] for j in range(4)])
            turn_tokens(0)
            tiles(pe, tile)

        @block.scalar
        def _(act):
            def normalise(i, p):
                act.wait_ge(factors3_ready, i + 1)
                if isinstance(i, int) and i == 0:
                    act.wait_ge(w_ready, OT)
                else:
                    act.wait_ge(turned_full[3], i + OT)
                nc.scalar.activation(xn3[:], x2[:, p, :], ACT.Identity, bias=nf3[:, 4:5],
                                     scale=nf3[:, 3:4]).then_inc(xn3_ready, 1)

            def token_high(i, p):
                for u in range(4):
                    act.wait_ge(turned_full[u], i + (OT + 1))
                    nc.scalar.copy(x_high[:, p, 4 * u:4 * u + 4, :].rearrange("p c n -> p (c n)"),
                                   bank[u][:]).then_inc(high_ready, 1)

            for t in range(OT):
                for u in range(4):
                    act.wait_ge(turned_full[u], t + 1)
                    nc.scalar.activation(w_high[:, 4 * u:4 * u + 4, t * P:(t + 1) * P],
                                         bank[u][:].rearrange("p (c n) -> p c n", n=P), ACT.Copy,
                                         scale=1.0 / LO).then_inc(high_ready, 1)
            normalise(0, 0)
            token_high(0, 0)

            def tile(i, p):
                if more(i):
                    normalise(i + 1, 1 - p)
                    token_high(i + 1, 1 - p)

            tiles(act, tile)

        @block.vector
        def _(dve):
            def stats(i, p):
                dve.wait_ge(x2_loaded[p], landed(i, p))
                wait(dve, factors3_ready, i)
                for d in range(DB):
                    nc.vector.bn_stats(bn3[:, d], x2[:, p, d * 512:(d + 1) * 512]).then_inc(bn3_step, 1)
                dve.wait_ge(bn3_step, (i + 1) * DB)
                pass_by(dve, dve_passed3)
                nc.vector.bn_aggr(mv3[:], bn3[:].rearrange("p d s -> p (d s)")).then_inc(stats3_ready, 1)

            def token_low(i, p):
                for u in range(4):
                    dve.wait_ge(high_ready, i * 4 + (4 * OT + u + 1))
                    part = slice(4 * u, 4 * u + 4)
                    nc.vector.tensor_tensor(x_low[:, p, part, :].rearrange("p c n -> p (c n)"), bank[u][:],
                                            x_high[:, p, part, :].rearrange("p c n -> p (c n)"),
                                            ALU.subtract).then_inc(turned_emptied[u], 1)
                nc.vector.tensor_scalar(x_small[:, p], x_high[:, p], 1.0 / LO, None,
                                        ALU.mult).then_inc(small_ready, 1)

            def scale(t):
                dve.wait_ge(w_loaded[t % 2], 16 * (t // 2 + 1))
                nc.vector.tensor_tensor(w_nat[:, t % 2, :].rearrange("p (g r) -> p g r", r=GROUP),
                                        w_nat[:, t % 2, :].bitcast(I32).rearrange("p (g r) -> p g r", r=GROUP),
                                        step_of[:, t, :].unsqueeze(2).broadcast_to((P, G, GROUP)),
                                        ALU.mult).then_inc(scaled, 1)

            def low(t):
                for u in range(4):
                    part = (slice(None), slice(4 * u, 4 * u + 4), slice(t * P, (t + 1) * P))
                    dve.wait_ge(high_ready, 4 * t + u + 1)
                    nc.vector.scalar_tensor_tensor(w_low[part], w_high[part], -LO,
                                                   bank[u][:].rearrange("p (c n) -> p c n", n=P),
                                                   ALU.mult, ALU.add).then_inc(turned_emptied[u], 1)

            dve.wait_ge(rng_loaded, 16)
            nc.vector.tensor_tensor(step_of, rng[:, :, :, 1], rng[:, :, :, 0], ALU.subtract).then_inc(range_step, 1)
            nc.vector.tensor_scalar(least_of, rng[:, :, :, 0], LO, None, ALU.mult).then_inc(ranges_ready, 1)
            dve.wait_ge(range_step, 1)
            nc.vector.tensor_scalar(step_of, step_of, LO / LEVELS, None, ALU.mult).then_inc(ranges_ready, 1)
            dve.wait_ge(ranges_ready, 2)
            scale(0)
            for t in range(OT):
                if t + 1 < OT:
                    scale(t + 1)
                low(t)
            stats(0, 0)
            token_low(0, 0)

            def tile(i, p):
                if more(i):
                    stats(i + 1, 1 - p)
                for d in range(DB):
                    if d == 2 and more(i):
                        token_low(i + 1, 1 - p)
                    dve.wait_ge(y_filled, i * DB + (d + 1))
                    dve.wait_ge(biased, i + 1)
                    part = x2[:, p, d * 512:(d + 1) * 512]
                    nc.vector.tensor_tensor(part, y[d][:], part, ALU.add).then_inc(y_emptied, 1)

            tiles(dve, tile)

        @block.gpsimd
        def _(pool):
            def add_bias(i, p):
                link = chain(pool, norm3_step, i * NORM_LINKS)
                pool.wait_ge(stats3_ready, i + 1)
                wait(pool, xn3_ready, i)
                norm_factors(nc, pool, link, mv3, nf3, consts).then_inc(factors3_ready, 1)
                pool.wait_ge(xn3_ready, i + 1)
                nc.gpsimd.tensor_tensor(x2[:, p, :], x2[:, p, :], bias_row[:], ALU.add).then_inc(biased, 1)

            pool.wait_ge(ranges_ready, 2)
            for t in range(OT):
                pool.wait_ge(scaled, t + 1)
                rows = w_nat[:, t % 2, :].rearrange("p (g r) -> p g r", r=GROUP)
                nc.gpsimd.tensor_tensor(rows, rows, least_of[:, t, :].unsqueeze(2).broadcast_to((P, G, GROUP)),
                                        ALU.add).then_inc(w_ready, 1)
            pool.wait_ge(bias_loaded, 16)
            add_bias(0, 0)

            def tile(i, p):
                if more(i):
                    add_bias(i + 1, 1 - p)

            tiles(pool, tile)


_INS = ["x", "ctx_4096", "L0_attn_Wq", "L0_attn_bq", "L0_attn_Wk", "L0_attn_bk", "L0_attn_Wv", "L0_attn_bv",
        "L0_ffn_weight_q3", "L0_ffn_weight_ranges", "L0_ffn_bias"]


def kernel(**inputs):
    import numpy as np
    import concourse.bacc as bacc
    from concourse.bass_utils import run_bass_kernel_spmd

    nc = bacc.Bacc("TRN2", target_bir_lowering=False, num_devices=1)
    arrays, args = {}, []
    for name in _INS:
        a = np.ascontiguousarray(inputs[name])
        arrays[name] = a
        args.append(nc.dram_tensor(name, a.shape, mybir.dt.from_np(a.dtype), kind="ExternalInput").ap())
    shape = arrays["x"].shape
    out = nc.dram_tensor("out", shape, F32, kind="ExternalOutput").ap()
    build(nc, *args, out)
    return run_bass_kernel_spmd(nc, [arrays], core_ids=[0]).results[0]["out"]
```

```python
from contextlib import ExitStack

import concourse.bass as bass
from concourse import mybir

F32 = mybir.dt.float32
F16 = mybir.dt.float16
BF16 = mybir.dt.bfloat16
I32 = mybir.dt.int32
ALU = mybir.AluOpType
ACT = mybir.ActivationFunctionType
AX = mybir.AxisListType

P = 128
EPS = 1e-5
LO = 2048.0


def wait(eng, sem, value):
    if isinstance(value, int) and value <= 0:
        return
    eng.wait_ge(sem, value)


def pass_by(eng, passed):
    eng.sem_inc(passed, 1)


def at(eng, value):
    return value if isinstance(value, int) else eng.snap(value)


def late(i, turns):
    return not isinstance(i, int) or i >= turns


def chain(eng, sem, base):
    state = [0]

    def link(instruction):
        state[0] += 1
        instruction.then_inc(sem, 1)
        eng.wait_ge(sem, base + state[0])

    return link


def build(nc, x, ctx_kv, Wq, bq, Wk, bk, Wv, bv, q3, ranges, bias, out):
    B, Q, D = x.shape
    K = ctx_kv.shape[1]
    DH, H = Wq.shape[1], Wq.shape[2]
    NB = P // Q
    NT = B // NB
    DC = D // P
    KC = K // P
    DB = D // 512
    CPB = 512 // P
    NW = 3 * DH
    GROUP = q3.shape[1]
    G = D // GROUP
    assert K == KC * P + 1 and D == DH * H and NT % 2 == 0

    x_tok = x.rearrange("b q d -> (b q) d")
    out_tok = out.rearrange("b q d -> (b q) d")
    x2_dram = nc.dram_tensor("x2_scratch", (B * Q, D), F32).ap()

    with ExitStack() as ctx:
        def sb(name, shape, dt):
            return ctx.enter_context(nc.sbuf_tensor(name, shape, dt))

        def sem(name):
            return ctx.enter_context(nc.semaphore(name))

        ident = sb("ident", [P, P], F32)
        consts = sb("consts", [P, len(NORM_CONSTS)], F32)
        consts_ready = sem("consts_ready")

        attention(nc, ident, consts, consts_ready, x_tok, ctx_kv, Wq, bq, Wk, bk, Wv, bv, x2_dram,
                  NT, NB, Q, D, DC, KC, DB, CPB, DH, H, NW)
        feed_forward(nc, ident, consts, x2_dram, q3, ranges, bias, out_tok, NT, D, DC, DB, CPB, GROUP, G)


def norm_factors(nc, pool, link, stats, factors, consts):
    v, y, a, r, nb = (factors[:, n:n + 1] for n in range(5))
    minus_half, eps, three_halves, minus_one = (consts[:, n:n + 1] for n in range(4))
    link(nc.gpsimd.tensor_tensor(v, stats[:, 1:2], eps, ALU.add))
    link(nc.gpsimd.tensor_tensor(y, v, minus_half, ALU.pow))
    link(nc.gpsimd.tensor_tensor(a, y, y, ALU.mult))
    link(nc.gpsimd.tensor_tensor(a, a, v, ALU.mult))
    link(nc.gpsimd.tensor_tensor(a, a, minus_half, ALU.mult))
    link(nc.gpsimd.tensor_tensor(a, a, three_halves, ALU.add))
    link(nc.gpsimd.tensor_tensor(r, y, a, ALU.mult))
    link(nc.gpsimd.tensor_tensor(a, stats[:, 0:1], r, ALU.mult))
    return nc.gpsimd.tensor_tensor(nb, a, minus_one, ALU.mult)


NORM_LINKS = 8
NORM_CONSTS = (-0.5, EPS, 1.5, -1.0)
CONSTS_READY = 6


def attention(nc, ident, consts, consts_ready, x_tok, ctx_kv, Wq, bq, Wk, bk, Wv, bv, x2_dram,
              NT, NB, Q, D, DC, KC, DB, CPB, DH, H, NW):
    SCALE = float(DH) ** -0.5
    NS = 4
    DS = DH // NS
    K0 = KC * P
    WRING = 2
    EXP_AFTER = (4, 8)
    with ExitStack() as ctx:
        def sb(name, shape, dt=F32):
            return ctx.enter_context(nc.sbuf_tensor(name, shape, dt))

        def psum(name, shape):
            return ctx.enter_context(nc.psum_tensor(name, shape, F32))

        def sem(name):
            return ctx.enter_context(nc.semaphore(name))

        keys = sb("keys", [P, DB, NB, KC, 512])
        last = sb("last", [P, 2, D])
        xa = sb("xa", [P, 2, D])
        xb = sb("xb", [P, 2, D])
        xn1 = sb("xn1", [P, D])
        xn2 = sb("xn2", [P, D])
        xn1T = sb("xn1T", [P, DC, P])
        xn2T = sb("xn2T", [P, DC, P])
        keysT = sb("keysT", [P, 4, NB, K0])
        wqkv = sb("wqkv", [P, DC, NW])
        x2 = sb("x2_out", [P, D])
        wstage = [x2[:], xb[:, 1, :]]
        bias_qkv = sb("bias_qkv", [P, NW])
        prod = sb("prod", [P, 2, DS, DH])
        junk = sb("junk", [P, D], BF16)
        probs = sb("probs", [P, K0])
        probsT = sb("probsT", [P, KC, P])
        qkv = sb("qkv", [P, 2, NW])
        bn1 = sb("bn1", [P, DB, 6])
        bn2 = sb("bn2", [P, DB, 6])
        mv1 = sb("mv1", [P, 2])
        mv2 = sb("mv2", [P, 2])
        nf1 = sb("nf1", [P, 5])
        nf2 = sb("nf2", [P, 5])
        s_last = sb("s_last", [P, 1])
        row = sb("row", [P, 8])
        kext = sb("kext", [P, 2])
        qlow = sb("qlow", [P, DH])
        top = sb("top", [P, 2, DH])
        den = sb("den", [P, DH])
        num = sb("num", [P, DH])
        rden = sb("rden", [P, DH])
        o = sb("o", [P, DH])

        bank = [psum(f"bank{n}", [P, 512]) for n in range(4)]
        scores = psum("scores", [P, 512])
        pvb = [psum(f"pv{n}", [P, 512]) for n in range(2)]
        qkv_sums = psum("qkv_sums", [P, 512])

        x_loaded = [sem(f"x_loaded{n}") for n in range(2)]
        last_loaded = [sem(f"last_loaded{n}") for n in range(2)]
        keys_loaded = [sem(f"keys_loaded{n}") for n in range(DB)]
        w_loaded = [sem(f"w_loaded{n}") for n in range(WRING)]
        small_loaded = sem("small_loaded")
        wkv_loaded = sem("wkv_loaded")
        w_summed = sem("w_summed")
        bank_full = [sem(f"bank_full{n}") for n in range(4)]
        bank_emptied = [sem(f"bank_emptied{n}") for n in range(4)]
        chunk_scored = sem("chunk_scored")
        qkv_done = sem("qkv_done")
        qkv_read = sem("qkv_read")
        probsT_done = sem("probsT_done")
        probsT_read = sem("probsT_read")
        pv_filled = sem("pv_filled")
        pv_emptied = sem("pv_emptied")
        stats1_ready = sem("stats1_ready")
        stats2_ready = sem("stats2_ready")
        factors1_ready = sem("factors1_ready")
        factors2_ready = sem("factors2_ready")
        xn1_ready = sem("xn1_ready")
        xn2_ready = sem("xn2_ready")
        last_scored = sem("last_scored")
        negmax_ready = sem("negmax_ready")
        probs_ready = sem("probs_ready")
        residual_ready = sem("residual_ready")
        top_ready = sem("top_ready")
        prod_ready = sem("prod_ready")
        exp_ready = sem("exp_ready")
        den_ready = sem("den_ready")
        weighted_ready = sem("weighted_ready")
        num_ready = sem("num_ready")
        o_ready = sem("o_ready")
        x2_ready = sem("x2_ready")
        x2_stored = sem("x2_stored")
        softmax_step = sem("softmax_step")
        dve_passed = sem("dve_passed")
        sp_passed = sem("sp_passed")
        top_step = sem("top_step")
        ext_step = sem("ext_step")
        bn1_step = sem("bn1_step")
        bn2_step = sem("bn2_step")
        rden_step = sem("rden_step")
        bias_step = sem("bias_step")
        outer_step = sem("outer_step")
        norm1_step = sem("norm1_step")
        norm2_step = sem("norm2_step")

        def xn1_use(i):
            return 1 if isinstance(i, int) and i == 0 else i * 10

        def pair_use(i, j):
            if isinstance(i, int) and i == 0:
                return j + 2
            return i * 10 + (j + 1 if j < 2 else j + 2)

        def xn2_use(i):
            return i * 10 + 3 if not isinstance(i, int) or i < NT else i * 10

        def tiles(eng, tile):
            tile(0, 0)
            tile(1, 1)
            with eng.Fori(1, NT // 2 - 1) as j:
                tile(j * 2, 0)
                tile(j * 2 + 1, 1)
            tile(NT - 2, 0)
            tile(NT - 1, 1)

        def landed(i, p):
            return i * 8 + (16 - 8 * p)

        block = ctx.enter_context(nc.Block())

        @block.sync
        def _(sp):
            def load_x(i, p, freed=0):
                row0 = at(sp, i * P)
                wait(sp, residual_ready, freed)
                sp.dma_start(xa[:, p, :], x_tok[bass.ds(row0, P), :]).then_inc(x_loaded[p], 16)

            def load_last(i, p):
                batch = [at(sp, i * NB + b) for b in range(NB)]
                wait(sp, residual_ready, i - 1)
                for b in range(NB):
                    sp.dma_start(last[b * Q:(b + 1) * Q, p, :],
                                 ctx_kv[bass.ds(batch[b], 1), K0, :].broadcast_to((Q, D))
                                 ).then_inc(last_loaded[p], 16)

            def load_keys(i):
                batch = [at(sp, i * NB + b) for b in range(NB)]
                for d in range(DB):
                    wait(sp, pv_filled, i * DB + (d + 1 - DB))
                    pass_by(sp, sp_passed)
                    for b in range(NB):
                        sp.dma_start(keys[:, d, b],
                                     ctx_kv[bass.ds(batch[b], 1), 0:K0, d * 512:(d + 1) * 512]
                                     .rearrange("a (c p) n -> p (a c) n", p=P)
                                     ).then_inc(keys_loaded[d], 16)

            def store_x2(m):
                row0 = at(sp, m * P)
                wait(sp, x2_ready, m + 1)
                sp.dma_start(x2_dram[bass.ds(row0, P), :], x2[:]).then_inc(x2_stored, 16)

            sp.sem_inc(x2_stored, 16)
            load_x(0, 0)
            load_keys(0)
            load_last(0, 0)
            load_x(1, 1)

            def tile(i, p):
                if not isinstance(i, int) or i + 1 < NT:
                    load_last(i + 1, 1 - p)
                if not isinstance(i, int) or i + 2 < NT:
                    load_x(i + 2, p, freed=i + 1)
                if not isinstance(i, int) or i + 1 < NT:
                    load_keys(i + 1)
                if late(i, 2):
                    store_x2(i - 2)

            tiles(sp, tile)
            store_x2(NT - 2)
            store_x2(NT - 1)
            sp.wait_ge(x2_stored, 16 * NT + 16)

        @block.tensor
        def _(pe):
            def turn(n, s, blocks):
                wait(pe, bank_emptied[s], n - 1)
                for j, block_in in enumerate(blocks):
                    mm = nc.tensor.transpose(bank[s][:, j * P:(j + 1) * P], block_in, ident[:])
                mm.then_inc(bank_full[s], 1)

            def turn_tokens(n, source):
                for u in range(4):
                    turn(n, u, [source[:, (4 * u + j) * P:(4 * u + j + 1) * P] for j in range(4)])

            def turn_chunk(i, c):
                if c % CPB == 0:
                    pe.wait_ge(keys_loaded[c // CPB], (i + 1) * (16 * NB))
                for h in range(2):
                    turn(pair_use(i, c // 2), 2 * (c % 2) + h,
                         [keys[:, c // CPB, 2 * h + b, kc, (c % CPB) * P:(c % CPB + 1) * P]
                          for b in range(2) for kc in range(KC)])

            def score_chunk(i, c):
                if c == 0:
                    wait(pe, probsT_read, i)
                if c % 4 == 0:
                    pe.wait_ge(bank_emptied[c // 4], xn1_use(i))
                for h in range(2):
                    pe.wait_ge(bank_emptied[2 * (c % 2) + h], pair_use(i, c // 2))
                for b in range(NB):
                    mm = nc.tensor.matmul(scores[b * Q:(b + 1) * Q, 0:K0], xn1T[:, c, b * Q:(b + 1) * Q],
                                          keysT[:, c % 4, b, :], start=(c == 0), stop=(c == DC - 1))
                mm.then_inc(chunk_scored, 1)

            def project(i):
                wait(pe, qkv_read, i - 1)
                for u in range(4):
                    pe.wait_ge(bank_emptied[u], xn2_use(i))
                for c in range(DC):
                    mm = nc.tensor.matmul(qkv_sums[:, 0:NW], xn2T[:, c, :], wqkv[:, c, :],
                                          start=(c == 0), stop=(c == DC - 1))
                mm.then_inc(qkv_done, 1)

            def turn_xn1(i):
                pe.wait_ge(xn1_ready, i + 1)
                turn_tokens(xn1_use(i), xn1)

            def tile(i, p):
                turn_chunk(i, 0)
                for c in range(DC):
                    if c + 1 < DC:
                        turn_chunk(i, c + 1)
                    if c + 1 == 3 and late(i, 1):
                        pe.wait_ge(xn2_ready, i)
                        turn_tokens(xn2_use(i), xn2)
                    score_chunk(i, c)
                if late(i, 1):
                    if isinstance(i, int) and i == 1:
                        pe.wait_ge(w_summed, DC)
                        pe.wait_ge(wkv_loaded, 32)
                    project(i)
                if not isinstance(i, int) or i + 1 < NT:
                    turn_xn1(i + 1)
                pe.wait_ge(probs_ready, (i + 1) * 2)
                for kc in range(KC):
                    mm = nc.tensor.transpose(scores[:, kc * P:(kc + 1) * P], probs[:, kc * P:(kc + 1) * P],
                                             ident[:])
                mm.then_inc(probsT_done, 1)
                pe.wait_ge(probsT_read, i + 1)
                for d in range(DB):
                    wait(pe, pv_emptied, i * DB + (d - 1))
                    for kc in range(KC):
                        for b in range(NB):
                            mm = nc.tensor.matmul(pvb[d % 2][b * Q:(b + 1) * Q, :],
                                                  probsT[:, kc, b * Q:(b + 1) * Q], keys[:, d, b, kc, :],
                                                  start=(kc == 0), stop=(kc == KC - 1))
                    mm.then_inc(pv_filled, 1)

            pe.wait_ge(consts_ready, CONSTS_READY)
            turn_xn1(0)
            tiles(pe, tile)
            pe.wait_ge(xn2_ready, NT)
            turn_tokens(xn2_use(NT), xn2)
            project(NT)

        @block.scalar
        def _(act):
            def empty(n, s, target):
                act.wait_ge(bank_full[s], n)
                nc.scalar.copy(target, bank[s][:]).then_inc(bank_emptied[s], 1)

            def empty_tokens(n, target):
                for u in range(4):
                    empty(n, u, target[:, 4 * u:4 * u + 4, :].rearrange("p c n -> p (c n)"))

            def exp_slice(m, s):
                act.wait_ge(prod_ready, m * NS + (s + 1))
                nc.scalar.activation(prod[:, s % 2], prod[:, s % 2], ACT.Exp, scale=SCALE).then_inc(exp_ready, 1)

            def empty_chunk(i, c):
                wait(act, chunk_scored, i * DC + (c - 3))
                for h in range(2):
                    empty(pair_use(i, c // 2), 2 * (c % 2) + h,
                          keysT[:, c % 4, 2 * h:2 * h + 2, :].rearrange("p b k -> p (b k)"))

            def tile(i, p):
                if late(i, 2):
                    exp_slice(i - 2, 0)
                    exp_slice(i - 2, 1)
                for c in range(DC):
                    empty_chunk(i, c)
                    if c == 3 and late(i, 1):
                        empty_tokens(xn2_use(i), xn2T)
                    if c in EXP_AFTER and late(i, 2):
                        exp_slice(i - 2, 2 + EXP_AFTER.index(c))
                act.wait_ge(negmax_ready, i + 1)
                wait(act, probsT_done, i)
                nc.scalar.activation(probs[:], scores[:, 0:K0], ACT.Exp, bias=row[:, 1:2],
                                     accum_out=row[:, 2:3]).then_inc(probs_ready, 1)
                nc.scalar.activation(row[:, 3:4], s_last[:], ACT.Exp, bias=row[:, 1:2]).then_inc(probs_ready, 1)
                if not isinstance(i, int) or i + 1 < NT:
                    empty_tokens(xn1_use(i + 1), xn1T)
                act.wait_ge(probsT_done, i + 1)
                nc.scalar.copy(probsT[:].rearrange("p c n -> p (c n)"), scores[:, 0:K0]).then_inc(probsT_read, 1)

            empty_tokens(xn1_use(0), xn1T)
            tiles(act, tile)
            empty_tokens(xn2_use(NT), xn2T)
            for m in (NT - 2, NT - 1):
                for s in range(NS):
                    exp_slice(m, s)

        @block.vector
        def _(dve):
            def stats1(i, p):
                dve.wait_ge(x_loaded[p], landed(i, p))
                wait(dve, factors1_ready, i)
                for d in range(DB):
                    nc.vector.bn_stats(bn1[:, d], xa[:, p, d * 512:(d + 1) * 512]).then_inc(bn1_step, 1)
                dve.wait_ge(bn1_step, (i + 1) * DB)
                pass_by(dve, dve_passed)
                nc.vector.bn_aggr(mv1[:], bn1[:].rearrange("p d s -> p (d s)")).then_inc(stats1_ready, 1)

            def normalise(i, factors_ready, xn_ready, target, source, factors):
                dve.wait_ge(factors_ready, i + 1)
                nc.vector.tensor_scalar(target, source, factors[:, 3:4], factors[:, 4:5], ALU.mult,
                                        ALU.add).then_inc(xn_ready, 1)

            def qkv_out(i, p):
                q, k = qkv[:, p, 0:DH], qkv[:, p, DH:2 * DH]
                dve.wait_ge(qkv_done, i)
                nc.vector.tensor_tensor(qkv[:, p], qkv_sums[:, 0:NW], bias_qkv[:], ALU.add).then_inc(qkv_read, 1)
                dve.wait_ge(qkv_read, i)
                nc.vector.tensor_reduce(kext[:, 0:1], k, AX.X, ALU.max).then_inc(ext_step, 1)
                nc.vector.tensor_reduce(kext[:, 1:2], k, AX.X, ALU.min).then_inc(ext_step, 1)
                dve.wait_ge(ext_step, i * 2)
                nc.vector.tensor_scalar(qlow[:], q, kext[:, 1:2], None, ALU.mult).then_inc(top_step, 1)
                dve.wait_ge(top_step, i)
                nc.vector.scalar_tensor_tensor(top[:, p], q, kext[:, 0:1], qlow[:],
                                               ALU.mult, ALU.max).then_inc(top_ready, 1)

            def sum_probs(m, s):
                dve.wait_ge(exp_ready, m * NS + (s + 1))
                nc.vector.tensor_reduce(den[:, s * DS:(s + 1) * DS], prod[:, s % 2], AX.X,
                                        ALU.add).then_inc(den_ready, 1)

            def sum_weighted(m, s):
                dve.wait_ge(weighted_ready, m * NS + (s + 1))
                nc.vector.tensor_reduce(num[:, s * DS:(s + 1) * DS], prod[:, s % 2], AX.X,
                                        ALU.add).then_inc(num_ready, 1)

            def finish_self(m):
                dve.wait_ge(den_ready, m * NS + NS)
                nc.vector.reciprocal(rden[:], den[:]).then_inc(rden_step, 1)
                dve.wait_ge(rden_step, m + 1)
                dve.wait_ge(num_ready, m * NS + NS)
                nc.vector.tensor_tensor(o[:], num[:], rden[:], ALU.mult).then_inc(o_ready, 1)

            def sum_heads(c):
                dve.wait_ge(w_loaded[c % WRING], 16 * (c // WRING + 1))
                nc.vector.tensor_reduce(wqkv[:, c, 0:DH],
                                        wstage[c % WRING].rearrange("p (d h) -> p d h", h=H),
                                        AX.X, ALU.add).then_inc(w_summed, 1)

            def score_last(i, p):
                dve.wait_ge(last_loaded[p], i * (8 * NB) + (16 - 8 * p) * NB)
                wait(dve, probs_ready, i * 2)
                nc.vector.tensor_tensor_reduce(out=junk[:], in0=xn1[:], in1=last[:, p, :], scale=1.0,
                                               scalar=0.0, op0=ALU.mult, op1=ALU.add,
                                               accum_out=s_last[:]).then_inc(last_scored, 1)

            def tile(i, p):
                link = chain(dve, softmax_step, i * 4)
                more = not isinstance(i, int) or i + 1 < NT
                if late(i, 2):
                    sum_probs(i - 2, 0)
                score_last(i, p)
                if late(i, 2):
                    sum_weighted(i - 2, 0)
                    sum_probs(i - 2, 1)
                    sum_weighted(i - 2, 1)
                if more:
                    stats1(i + 1, 1 - p)
                if late(i, 2):
                    sum_probs(i - 2, 2)
                    sum_weighted(i - 2, 2)
                if more:
                    dve.wait_ge(bank_full[3], xn1_use(i))
                    dve.wait_ge(last_scored, i + 1)
                    normalise(i + 1, factors1_ready, xn1_ready, xn1[:], xa[:, 1 - p, :], nf1)
                if isinstance(i, int) and i == 1:
                    for c in range(DC):
                        sum_heads(c)
                if late(i, 2):
                    sum_probs(i - 2, 3)
                    sum_weighted(i - 2, 3)
                    finish_self(i - 2)
                dve.wait_ge(chunk_scored, (i + 1) * DC)
                wait(dve, probs_ready, i * 2)
                link(nc.vector.tensor_reduce(row[:, 0:1], scores[:, 0:K0], AX.X, ALU.max))
                dve.wait_ge(last_scored, i + 1)
                nc.vector.tensor_scalar(row[:, 1:2], row[:, 0:1], s_last[:], -1.0, ALU.max,
                                        ALU.mult).then_inc(negmax_ready, 1)
                dve.wait_ge(probs_ready, (i + 1) * 2)
                link(nc.vector.tensor_tensor(row[:, 4:5], row[:, 2:3], row[:, 3:4], ALU.add))
                link(nc.vector.reciprocal(row[:, 5:6], row[:, 4:5]))
                link(nc.vector.tensor_tensor(row[:, 6:7], row[:, 3:4], row[:, 5:6], ALU.mult))
                wait(dve, x2_ready, i - 1)
                nc.vector.scalar_tensor_tensor(xb[:, p, :], last[:, p, :], row[:, 6:7], xa[:, p, :], ALU.mult,
                                               ALU.add).then_inc(residual_ready, 1)
                if late(i, 1):
                    qkv_out(i, 1 - p)
                dve.wait_ge(residual_ready, i + 1)
                wait(dve, factors2_ready, i)
                for d in range(DB):
                    part = xb[:, p, d * 512:(d + 1) * 512]
                    dve.wait_ge(pv_filled, i * DB + (d + 1))
                    nc.vector.scalar_tensor_tensor(part, pvb[d % 2][:], row[:, 5:6], part, ALU.mult,
                                                   ALU.add).then_inc(pv_emptied, 1)
                    dve.wait_ge(pv_emptied, i * DB + (d + 1))
                    nc.vector.bn_stats(bn2[:, d], part).then_inc(bn2_step, 1)
                dve.wait_ge(bn2_step, (i + 1) * DB)
                pass_by(dve, dve_passed)
                nc.vector.bn_aggr(mv2[:], bn2[:].rearrange("p d s -> p (d s)")).then_inc(stats2_ready, 1)
                if late(i, 1):
                    dve.wait_ge(bank_full[3], xn2_use(i))
                normalise(i, factors2_ready, xn2_ready, xn2[:], xb[:, p, :], nf2)

            stats1(0, 0)
            normalise(0, factors1_ready, xn1_ready, xn1[:], xa[:, 0, :], nf1)
            dve.wait_ge(small_loaded, 48)
            nc.vector.tensor_reduce(bias_qkv[:, 0:DH], xn2[:].rearrange("p (d h) -> p d h", h=H), AX.X,
                                    ALU.add).then_inc(bias_step, 1)
            dve.wait_ge(bias_step, 1)
            tiles(dve, tile)
            for m in (NT - 2, NT - 1):
                for s in range(NS):
                    sum_probs(m, s)
                    sum_weighted(m, s)
                finish_self(m)
                if m == NT - 2:
                    qkv_out(NT, 1)

        @block.gpsimd
        def _(pool):
            def factors(i, step, mv, nf, stats_ready, factors_ready, xn_ready):
                link = chain(pool, step, i * NORM_LINKS)
                pool.wait_ge(stats_ready, i + 1)
                wait(pool, xn_ready, i)
                norm_factors(nc, pool, link, mv, nf, consts).then_inc(factors_ready, 1)

            def product(m, p, s):
                n = m * NS + (s + 1)
                if s >= 2:
                    pool.wait_ge(num_ready, n - 2)
                S = prod[:, s % 2]
                nc.gpsimd.tensor_tensor(S, qkv[:, p, s * DS:(s + 1) * DS].unsqueeze(2).broadcast_to((P, DS, DH)),
                                        qkv[:, p, DH:2 * DH].unsqueeze(1).broadcast_to((P, DS, DH)),
                                        ALU.mult).then_inc(outer_step, 1)
                pool.wait_ge(outer_step, n)
                nc.gpsimd.tensor_tensor(S, S, top[:, p, s * DS:(s + 1) * DS].unsqueeze(2)
                                        .broadcast_to((P, DS, DH)), ALU.subtract).then_inc(prod_ready, 1)

            def weigh(m, p, s):
                pool.wait_ge(den_ready, m * NS + (s + 1))
                S = prod[:, s % 2]
                nc.gpsimd.tensor_tensor(S, S, qkv[:, p, 2 * DH:3 * DH].unsqueeze(1).broadcast_to((P, DS, DH)),
                                        ALU.mult).then_inc(weighted_ready, 1)

            def first_products(m, p):
                pool.wait_ge(top_ready, m + 1)
                product(m, p, 0)
                product(m, p, 1)

            def add_self(m, p):
                pool.wait_ge(o_ready, m + 1)
                pool.wait_ge(x2_stored, m * 16 + 16)
                nc.gpsimd.tensor_tensor(x2[:].rearrange("p (d h) -> p d h", h=H),
                                        xb[:, p, :].rearrange("p (d h) -> p d h", h=H),
                                        o[:].unsqueeze(2).broadcast_to((P, DH, H)),
                                        ALU.add).then_inc(x2_ready, 1)

            def tile(i, p):
                if late(i, 2):
                    weigh(i - 2, p, 0)
                    product(i - 2, p, 2)
                    weigh(i - 2, p, 1)
                    product(i - 2, p, 3)
                if not isinstance(i, int) or i + 1 < NT:
                    factors(i + 1, norm1_step, mv1, nf1, stats1_ready, factors1_ready, xn1_ready)
                if late(i, 2):
                    weigh(i - 2, p, 2)
                    weigh(i - 2, p, 3)
                    add_self(i - 2, p)
                first_products(i - 1, 1 - p)
                factors(i, norm2_step, mv2, nf2, stats2_ready, factors2_ready, xn2_ready)

            nc.gpsimd.memset(ident[:], 0.0).then_inc(consts_ready, 1)
            for n, value in enumerate(NORM_CONSTS):
                nc.gpsimd.memset(consts[:, n:n + 1], value).then_inc(consts_ready, 1)
            pool.wait_ge(consts_ready, CONSTS_READY - 1)
            nc.gpsimd.affine_select(out=ident[:], in_=ident[:], compare_op=ALU.not_equal, fill=1.0, base=0,
                                    pattern=[[-1, P]], channel_multiplier=1).then_inc(consts_ready, 1)
            pool.dma_start(xn2[:], bq.rearrange("d h -> (d h)").unsqueeze(0).broadcast_to((P, DH * H))
                           ).then_inc(small_loaded, 16)
            pool.dma_start(bias_qkv[:, DH:2 * DH], bk.rearrange("d o -> o d").broadcast_to((P, DH))
                           ).then_inc(small_loaded, 16)
            pool.dma_start(bias_qkv[:, 2 * DH:3 * DH], bv.rearrange("d o -> o d").broadcast_to((P, DH))
                           ).then_inc(small_loaded, 16)

            def load_w(c):
                wait(pool, w_summed, c - WRING + 1)
                pool.dma_start(wstage[c % WRING], Wq[c * P:(c + 1) * P].rearrange("p d h -> p (d h)")
                               ).then_inc(w_loaded[c % WRING], 16)

            factors(0, norm1_step, mv1, nf1, stats1_ready, factors1_ready, xn1_ready)
            factors(1, norm1_step, mv1, nf1, stats1_ready, factors1_ready, xn1_ready)
            pool.dma_start(wqkv[:, :, DH:2 * DH], Wk.rearrange("(c p) d o -> p c (d o)", p=P)
                           ).then_inc(wkv_loaded, 16)
            pool.dma_start(wqkv[:, :, 2 * DH:3 * DH], Wv.rearrange("(c p) d o -> p c (d o)", p=P)
                           ).then_inc(wkv_loaded, 16)
            for c in range(WRING):
                load_w(c)
            factors(0, norm2_step, mv2, nf2, stats2_ready, factors2_ready, xn2_ready)
            factors(2, norm1_step, mv1, nf1, stats1_ready, factors1_ready, xn1_ready)
            for c in range(WRING, DC):
                load_w(c)
            first_products(0, 0)
            factors(1, norm2_step, mv2, nf2, stats2_ready, factors2_ready, xn2_ready)
            with pool.Fori(1, NT // 2 - 1) as j:
                tile(j * 2, 0)
                tile(j * 2 + 1, 1)
            tile(NT - 2, 0)
            tile(NT - 1, 1)
            for m, p in ((NT - 2, 0), (NT - 1, 1)):
                if m == NT - 1:
                    first_products(m, p)
                for s in range(NS):
                    weigh(m, p, s)
                    if s + 2 < NS:
                        product(m, p, s + 2)
                add_self(m, p)


def feed_forward(nc, ident, consts, x2_dram, q3, ranges, bias, out_tok, NT, D, DC, DB, CPB, GROUP, G):
    LEVELS = 7.0
    OT = D // P
    with ExitStack() as ctx:
        def sb(name, shape, dt=F32):
            return ctx.enter_context(nc.sbuf_tensor(name, shape, dt))

        def sem(name):
            return ctx.enter_context(nc.semaphore(name))

        w_high = sb("w_high", [P, DC, D], F16)
        w_low = sb("w_low", [P, DC, D], F16)
        bias_row = sb("bias_row", [P, D], F16)
        w_nat = sb("w_nat", [P, 2, D])
        x2 = sb("x2", [P, 2, D])
        xn3 = sb("xn3", [P, D])
        rng = w_nat[:, 1, :].bitcast(F16)[:, 0:OT * G * 2].rearrange("p (t g r) -> p t g r", g=G, r=2)
        step_of = sb("step_of", [P, OT, G])
        least_of = sb("least_of", [P, OT, G])
        x_high = sb("x_high", [P, 2, DC, P], F16)
        x_low = sb("x_low", [P, 2, DC, P], F16)
        x_small = sb("x_small", [P, 2, DC, P], F16)
        bn3 = sb("bn3", [P, DB, 6])
        mv3 = sb("mv3", [P, 2])
        nf3 = sb("nf3", [P, 5])
        bank = [ctx.enter_context(nc.psum_tensor(f"turned{n}", [P, 512], F32)) for n in range(4)]
        y = [ctx.enter_context(nc.psum_tensor(f"y{n}", [P, 512], F32)) for n in range(DB)]

        rng_loaded = sem("rng_loaded")
        bias_loaded = sem("bias_loaded")
        w_loaded = [sem(f"rows_loaded{n}") for n in range(2)]
        x2_loaded = [sem(f"x2_loaded{n}") for n in range(2)]
        out_stored = [sem(f"out_stored{n}") for n in range(2)]
        range_step = sem("range_step")
        ranges_ready = sem("ranges_ready")
        scaled = sem("scaled")
        w_ready = sem("w_ready")
        turned_full = [sem(f"turned_full{n}") for n in range(4)]
        high_ready = sem("high_ready")
        turned_emptied = [sem(f"turned_emptied{n}") for n in range(4)]
        small_ready = sem("small_ready")
        bn3_step = sem("bn3_step")
        dve_passed3 = sem("dve_passed3")
        stats3_ready = sem("stats3_ready")
        norm3_step = sem("norm3_step")
        factors3_ready = sem("factors3_ready")
        xn3_ready = sem("xn3_ready")
        biased = sem("biased")
        y_filled = sem("y_filled")
        y_emptied = sem("y_emptied")

        TPB = CPB

        def tiles(eng, tile):
            with eng.Fori(1, NT // 2 - 1) as j:
                tile(j * 2, 0)
                tile(j * 2 + 1, 1)
            tile(NT - 2, 0)
            tile(NT - 1, 1)

        def more(i):
            return not isinstance(i, int) or i + 1 < NT

        def landed(i, p):
            return i * 8 + (16 - 8 * p)

        def rows_use(t):
            return t + 1 if t < TPB else t + 3

        def token_use(i):
            return TPB + 1 + i if isinstance(i, int) and i < 2 else i + (OT + 1)

        block = ctx.enter_context(nc.Block())

        @block.sync
        def _(sp):
            q_rows = q3.rearrange("(t p g) r -> t p (g r)", p=P, g=G)

            def load_x2(i, p, freed=None):
                row0 = at(sp, i * P)
                if freed is not None:
                    sp.wait_ge(*freed)
                sp.dma_start(x2[:, p, :], x2_dram[bass.ds(row0, P), :]).then_inc(x2_loaded[p], 16)

            def store(i, p, count):
                row0 = at(sp, i * P)
                sp.wait_ge(y_emptied, count)
                sp.dma_start(out_tok[bass.ds(row0, P), :], x2[:, p, :]).then_inc(out_stored[p], 16)

            def load_rows(t):
                if t == 1:
                    sp.wait_ge(ranges_ready, 2)
                elif t > 1:
                    sp.wait_ge(turned_full[3], rows_use(t - 2))
                sp.dma_start(w_nat[:, t % 2, :].bitcast(I32), q_rows[t]).then_inc(w_loaded[t % 2], 16)

            sp.dma_start(rng.rearrange("p t g r -> p t (g r)"),
                         ranges.rearrange("(t p g) r -> p t (g r)", p=P, g=G)).then_inc(rng_loaded, 16)
            load_rows(0)
            load_rows(1)
            for p in range(2):
                load_x2(p, p)
            sp.dma_start(bias_row[:], bias.unsqueeze(0).broadcast_to((P, D))).then_inc(bias_loaded, 16)
            for t in range(2, OT):
                load_rows(t)
            store(0, 0, 2 * DB - 1)
            load_x2(2, 0, freed=(out_stored[0], 16))

            def tile(i, p):
                store(i - 1, 1 - p, i * DB)
                if more(i):
                    load_x2(i + 1, 1 - p, freed=(out_stored[1 - p], landed(i - 1, 1 - p)))

            tiles(sp, tile)
            store(NT - 1, 1, NT * DB)
            for p in range(2):
                sp.wait_ge(out_stored[p], 16 * (NT // 2))

        @block.tensor
        def _(pe):
            def turn(n, s, blocks):
                wait(pe, turned_emptied[s], n - 1)
                for j, block_in in enumerate(blocks):
                    mm = nc.tensor.transpose(bank[s][:, j * P:(j + 1) * P], block_in, ident[:])
                mm.then_inc(turned_full[s], 1)

            def turn_tokens(i):
                pe.wait_ge(xn3_ready, i + 1)
                for u in range(4):
                    turn(token_use(i), u, [xn3[:, (4 * u + j) * P:(4 * u + j + 1) * P] for j in range(4)])

            def turn_rows(t):
                pe.wait_ge(w_ready, t + 1)
                for u in range(4):
                    turn(rows_use(t), u, [w_nat[:, t % 2, (4 * u + j) * P:(4 * u + j + 1) * P] for j in range(4)])

            def product(p, d, bank_of, filled):
                wait(pe, y_emptied, filled - (DB - 1))
                cols = slice(d * 512, (d + 1) * 512)
                for c in range(DC):
                    nc.tensor.matmul(y[bank_of][:], x_high[:, p, c, :], w_high[:, c, cols],
                                     start=(c == 0), stop=False)
                    nc.tensor.matmul(y[bank_of][:], x_low[:, p, c, :], w_high[:, c, cols],
                                     start=False, stop=False)
                    mm = nc.tensor.matmul(y[bank_of][:], x_small[:, p, c, :], w_low[:, c, cols],
                                          start=False, stop=(c == DC - 1))
                mm.then_inc(y_filled, 1)

            for t in range(TPB):
                turn_rows(t)
            turn_tokens(0)
            turn_tokens(1)
            for d in range(DB):
                for u in range(4):
                    pe.wait_ge(turned_emptied[u], rows_use(TPB * (d + 1) - 1))
                for p in range(2):
                    pe.wait_ge(small_ready, p + 1)
                    product(p, d, (2 * d + p) % DB, 2 * d + p)
                    if d + 1 < DB:
                        turn_rows(TPB * (d + 1) + 2 * p)
                        turn_rows(TPB * (d + 1) + 2 * p + 1)
            turn_tokens(2)

            def tile(i, p):
                pe.wait_ge(small_ready, i + 1)
                for d in range(DB):
                    if d == 2 and more(i):
                        turn_tokens(i + 1)
                    product(p, d, d, i * DB + d)

            tiles(pe, tile)

        @block.scalar
        def _(act):
            def token_high(i, p):
                for u in range(4):
                    act.wait_ge(turned_full[u], token_use(i))
                    nc.scalar.copy(x_high[:, p, 4 * u:4 * u + 4, :].rearrange("p c n -> p (c n)"),
                                   bank[u][:]).then_inc(high_ready, 1)

            def rows_high(t):
                for u in range(4):
                    act.wait_ge(turned_full[u], rows_use(t))
                    nc.scalar.activation(w_high[:, 4 * u:4 * u + 4, t * P:(t + 1) * P],
                                         bank[u][:].rearrange("p (c n) -> p c n", n=P), ACT.Copy,
                                         scale=1.0 / LO).then_inc(high_ready, 1)

            for t in range(TPB):
                rows_high(t)
            token_high(0, 0)
            token_high(1, 1)
            for t in range(TPB, OT):
                rows_high(t)
            token_high(2, 0)

            def tile(i, p):
                if more(i):
                    token_high(i + 1, 1 - p)

            tiles(act, tile)

        @block.vector
        def _(dve):
            def stats(i, p):
                dve.wait_ge(x2_loaded[p], landed(i, p))
                wait(dve, factors3_ready, i)
                for d in range(DB):
                    nc.vector.bn_stats(bn3[:, d], x2[:, p, d * 512:(d + 1) * 512]).then_inc(bn3_step, 1)
                dve.wait_ge(bn3_step, (i + 1) * DB)
                pass_by(dve, dve_passed3)
                nc.vector.bn_aggr(mv3[:], bn3[:].rearrange("p d s -> p (d s)")).then_inc(stats3_ready, 1)

            def normalise(i, p):
                dve.wait_ge(factors3_ready, i + 1)
                if late(i, 1):
                    dve.wait_ge(turned_full[3], token_use(i - 1) if isinstance(i, int) else i + OT)
                nc.vector.tensor_scalar(xn3[:], x2[:, p, :], nf3[:, 3:4], nf3[:, 4:5], ALU.mult,
                                        ALU.add).then_inc(xn3_ready, 1)

            def token_low(i, p):
                for u in range(4):
                    dve.wait_ge(high_ready, 4 * (token_use(i) - 1) + u + 1 if isinstance(i, int)
                                else i * 4 + (4 * OT + u + 1))
                    part = slice(4 * u, 4 * u + 4)
                    nc.vector.tensor_tensor(x_low[:, p, part, :].rearrange("p c n -> p (c n)"), bank[u][:],
                                            x_high[:, p, part, :].rearrange("p c n -> p (c n)"),
                                            ALU.subtract).then_inc(turned_emptied[u], 1)
                nc.vector.tensor_scalar(x_small[:, p], x_high[:, p], 1.0 / LO, None,
                                        ALU.mult).then_inc(small_ready, 1)

            def scale_rows(t):
                dve.wait_ge(w_loaded[t % 2], 16 * (t // 2 + 1))
                nc.vector.tensor_tensor(w_nat[:, t % 2, :].rearrange("p (g r) -> p g r", r=GROUP),
                                        w_nat[:, t % 2, :].bitcast(I32).rearrange("p (g r) -> p g r", r=GROUP),
                                        step_of[:, t, :].unsqueeze(2).broadcast_to((P, G, GROUP)),
                                        ALU.mult).then_inc(scaled, 1)

            def rows_low(t):
                for u in range(4):
                    part = (slice(None), slice(4 * u, 4 * u + 4), slice(t * P, (t + 1) * P))
                    dve.wait_ge(high_ready, 4 * (rows_use(t) - 1) + u + 1)
                    nc.vector.scalar_tensor_tensor(w_low[part], w_high[part], -LO,
                                                   bank[u][:].rearrange("p (c n) -> p c n", n=P),
                                                   ALU.mult, ALU.add).then_inc(turned_emptied[u], 1)

            def add_residual(p, d, bank_of, filled):
                dve.wait_ge(y_filled, filled)
                part = x2[:, p, d * 512:(d + 1) * 512]
                nc.vector.tensor_tensor(part, y[bank_of][:], part, ALU.add).then_inc(y_emptied, 1)

            dve.wait_ge(rng_loaded, 16)
            nc.vector.tensor_tensor(step_of[:], rng[:, :, :, 1], rng[:, :, :, 0], ALU.subtract).then_inc(range_step, 1)
            nc.vector.tensor_scalar(least_of[:], rng[:, :, :, 0], LO, None, ALU.mult).then_inc(ranges_ready, 1)
            dve.wait_ge(range_step, 1)
            nc.vector.tensor_scalar(step_of[:], step_of[:], LO / LEVELS, None, ALU.mult).then_inc(ranges_ready, 1)
            dve.wait_ge(ranges_ready, 2)
            scale_rows(0)
            for t in range(TPB):
                scale_rows(t + 1)
                rows_low(t)
                if t < 2:
                    stats(t, t)
                    if t == 0:
                        normalise(0, 0)
            token_low(0, 0)
            normalise(1, 1)
            token_low(1, 1)
            for d in range(DB):
                for p in range(2):
                    if d + 1 < DB:
                        for t in (TPB * (d + 1) + 2 * p, TPB * (d + 1) + 2 * p + 1):
                            if t + 1 < OT:
                                scale_rows(t + 1)
                            rows_low(t)
                    if d == 0:
                        dve.wait_ge(biased, p + 1)
                    add_residual(p, d, (2 * d + p) % DB, 2 * d + p + 1)
            stats(2, 0)
            normalise(2, 0)
            token_low(2, 0)

            def tile(i, p):
                if more(i):
                    stats(i + 1, 1 - p)
                    normalise(i + 1, 1 - p)
                dve.wait_ge(biased, i + 1)
                for d in range(DB):
                    if d == 2 and more(i):
                        token_low(i + 1, 1 - p)
                    add_residual(p, d, d, i * DB + (d + 1))

            tiles(dve, tile)

        @block.gpsimd
        def _(pool):
            def factors(i):
                link = chain(pool, norm3_step, i * NORM_LINKS)
                pool.wait_ge(stats3_ready, i + 1)
                wait(pool, xn3_ready, i)
                norm_factors(nc, pool, link, mv3, nf3, consts).then_inc(factors3_ready, 1)

            def add_bias(i, p):
                pool.wait_ge(xn3_ready, i + 1)
                nc.gpsimd.tensor_tensor(x2[:, p, :], x2[:, p, :], bias_row[:], ALU.add).then_inc(biased, 1)

            def add_least(t):
                pool.wait_ge(scaled, t + 1)
                rows = w_nat[:, t % 2, :].rearrange("p (g r) -> p g r", r=GROUP)
                nc.gpsimd.tensor_tensor(rows, rows, least_of[:, t, :].unsqueeze(2).broadcast_to((P, G, GROUP)),
                                        ALU.add).then_inc(w_ready, 1)

            pool.wait_ge(ranges_ready, 2)
            add_least(0)
            add_least(1)
            factors(0)
            add_least(2)
            add_least(3)
            factors(1)
            add_least(4)
            pool.wait_ge(bias_loaded, 16)
            add_bias(0, 0)
            add_bias(1, 1)
            for t in range(TPB + 1, OT):
                add_least(t)
            factors(2)
            add_bias(2, 0)

            def tile(i, p):
                if more(i):
                    factors(i + 1)
                    add_bias(i + 1, 1 - p)

            tiles(pool, tile)


_INS = ["x", "ctx_4096", "L0_attn_Wq", "L0_attn_bq", "L0_attn_Wk", "L0_attn_bk", "L0_attn_Wv", "L0_attn_bv",
        "L0_ffn_weight_q3", "L0_ffn_weight_ranges", "L0_ffn_bias"]


def kernel(**inputs):
    import numpy as np
    import concourse.bacc as bacc
    from concourse.bass_utils import run_bass_kernel_spmd

    nc = bacc.Bacc("TRN2", target_bir_lowering=False, num_devices=1)
    arrays, args = {}, []
    for name in _INS:
        a = np.ascontiguousarray(inputs[name])
        arrays[name] = a
        args.append(nc.dram_tensor(name, a.shape, mybir.dt.from_np(a.dtype), kind="ExternalInput").ap())
    shape = arrays["x"].shape
    out = nc.dram_tensor("out", shape, F32, kind="ExternalOutput").ap()
    build(nc, *args, out)
    return run_bass_kernel_spmd(nc, [arrays], core_ids=[0]).results[0]["out"]
```

```python
from contextlib import ExitStack

import concourse.bass as bass
from concourse import mybir

F32 = mybir.dt.float32
F16 = mybir.dt.float16
BF16 = mybir.dt.bfloat16
I32 = mybir.dt.int32
NS = 4
LEVELS = 7.0
ALU = mybir.AluOpType
ACT = mybir.ActivationFunctionType
AX = mybir.AxisListType

P = 128
EPS = 1e-5
LO = 2048.0


class Shared:

    def __init__(self, xa, x2, last, row_slots, xb, w_low_last, prod, w_high_last, keysT, w_high_2, xn1T,
                 step_of, least_of, rng, qkv, top, den, num, rden, o, q_rows, ranges, rng_loaded, rows_loaded,
                 range_step, ranges_ready, scaled, w_ready):
        self.xa, self.x2 = xa, x2
        self.last, self.row_slots = last, row_slots
        self.xb, self.w_low_last = xb, w_low_last
        self.prod, self.w_high_last = prod, w_high_last
        self.keysT, self.w_high_2 = keysT, w_high_2
        self.xn1T, self.step_of, self.least_of, self.rng = xn1T, step_of, least_of, rng
        self.qkv, self.top, self.den, self.num, self.rden, self.o = qkv, top, den, num, rden, o
        self.q_rows, self.ranges = q_rows, ranges
        self.rng_loaded, self.rows_loaded = rng_loaded, rows_loaded
        self.range_step, self.ranges_ready = range_step, ranges_ready
        self.scaled, self.w_ready = scaled, w_ready


def wait(eng, sem, value):
    if isinstance(value, int) and value <= 0:
        return
    eng.wait_ge(sem, value)


def pass_by(eng, passed):
    eng.sem_inc(passed, 1)


def at(eng, value):
    return value if isinstance(value, int) else eng.snap(value)


def late(i, turns):
    return not isinstance(i, int) or i >= turns


def chain(eng, sem, base):
    state = [0]

    def link(instruction):
        state[0] += 1
        instruction.then_inc(sem, 1)
        eng.wait_ge(sem, base + state[0])

    return link


def build(nc, x, ctx_kv, Wq, bq, Wk, bk, Wv, bv, q3, ranges, bias, out):
    B, Q, D = x.shape
    K = ctx_kv.shape[1]
    DH, H = Wq.shape[1], Wq.shape[2]
    NB = P // Q
    NT = B // NB
    DC = D // P
    KC = K // P
    DB = D // 512
    CPB = 512 // P
    NW = 3 * DH
    GROUP = q3.shape[1]
    G = D // GROUP
    assert K == KC * P + 1 and D == DH * H and NT % 2 == 0

    x_tok = x.rearrange("b q d -> (b q) d")
    out_tok = out.rearrange("b q d -> (b q) d")
    x2_dram = nc.dram_tensor("x2_scratch", (B * Q, D), F32).ap()

    with ExitStack() as ctx:
        def sb(name, shape, dt):
            return ctx.enter_context(nc.sbuf_tensor(name, shape, dt))

        def sem(name):
            return ctx.enter_context(nc.semaphore(name))

        ident = sb("ident", [P, P], F32)
        consts = sb("consts", [P, len(NORM_CONSTS)], F32)
        consts_ready = sem("consts_ready")
        OT = D // P
        xa = sb("xa", [P, 2, D], F32)
        last = sb("last", [P, 2, D], F32)
        xb = sb("xb", [P, 2, D], F32)
        prod = sb("prod", [P, 2 * D], F32)
        xn1T = sb("xn1T", [P, DC, P], F32)
        keysT = sb("keysT", [P, 2 * D], F32)
        steps = xn1T[:].rearrange("p c n -> p (c n)")
        shared = Shared(
            xa=xa, x2=xa,
            last=last, row_slots=([last[:, n, :] for n in range(2)]
                                  + [keysT[:, n * D:(n + 1) * D] for n in range(2)]),
            xb=xb, w_low_last=xb[:].rearrange("p a d -> p (a d)").bitcast(F16)
                               .rearrange("p (c n) -> p c n", n=512),
            prod=prod[:].rearrange("p (s q k) -> p s q k", s=NS, k=DH),
            w_high_last=prod[:].bitcast(F16).rearrange("p (c n) -> p c n", n=512),
            keysT=keysT[:], w_high_2=keysT[:].bitcast(F16).rearrange("p (c n) -> p c n", n=512),
            xn1T=xn1T,
            step_of=steps[:, 0:OT * G].rearrange("p (t g) -> p t g", g=G),
            least_of=steps[:, OT * G:2 * OT * G].rearrange("p (t g) -> p t g", g=G),
            rng=xa[:, 0, :].bitcast(F16)[:, 0:OT * G * 2].rearrange("p (t g r) -> p t g r", g=G, r=2),
            qkv=sb("qkv", [P, 2, 3 * DH], F32),
            top=sb("top", [P, 2, DH], F32),
            den=sb("den", [P, DH], F32),
            num=sb("num", [P, DH], F32),
            rden=sb("rden", [P, DH], F32),
            o=sb("o", [P, DH], F32),
            q_rows=q3.rearrange("(t p g) r -> t p (g r)", p=P, g=G),
            ranges=ranges.rearrange("(t p g) r -> p t g r", p=P, g=G),
            rng_loaded=sem("rng_loaded"),
            rows_loaded=[sem(f"rows_loaded{n}") for n in range(4)],
            range_step=sem("range_step"),
            ranges_ready=sem("ranges_ready"),
            scaled=sem("scaled"),
            w_ready=sem("w_ready"))

        attention(nc, ident, consts, consts_ready, x_tok, ctx_kv, Wq, bq, Wk, bk, Wv, bv, x2_dram, shared,
                  NT, NB, Q, D, DC, KC, DB, CPB, DH, H, NW, GROUP, G)
        feed_forward(nc, ident, consts, x2_dram, bias, out_tok, shared, NT, D, DC, DB, CPB, DH, H, GROUP, G)


EARLY_ROWS = 8


def row_slot(t):
    return t % 4 if t < EARLY_ROWS else t % 2


def rows_landed(t):
    return 16 * (t // 4 + 1 if t < EARLY_ROWS else (t - EARLY_ROWS) // 2 + EARLY_ROWS // 4 + 1)


def scale_rows(nc, dve, w, t, GROUP, G):
    rows = w.row_slots[row_slot(t)]
    dve.wait_ge(w.rows_loaded[row_slot(t)], rows_landed(t))
    nc.vector.tensor_tensor(rows.rearrange("p (g r) -> p g r", r=GROUP),
                            rows.bitcast(I32).rearrange("p (g r) -> p g r", r=GROUP),
                            w.step_of[:, t, :].unsqueeze(2).broadcast_to((P, G, GROUP)),
                            ALU.mult).then_inc(w.scaled, 1)


def add_least(nc, pool, w, t, GROUP, G):
    pool.wait_ge(w.scaled, t + 1)
    rows = w.row_slots[row_slot(t)].rearrange("p (g r) -> p g r", r=GROUP)
    nc.gpsimd.tensor_tensor(rows, rows, w.least_of[:, t, :].unsqueeze(2).broadcast_to((P, G, GROUP)),
                            ALU.add).then_inc(w.w_ready, 1)


def norm_factors(nc, pool, link, stats, factors, consts):
    v, y, a, r, nb = (factors[:, n:n + 1] for n in range(5))
    minus_half, eps, three_halves, minus_one = (consts[:, n:n + 1] for n in range(4))
    link(nc.gpsimd.tensor_tensor(v, stats[:, 1:2], eps, ALU.add))
    link(nc.gpsimd.tensor_tensor(y, v, minus_half, ALU.pow))
    link(nc.gpsimd.tensor_tensor(a, y, y, ALU.mult))
    link(nc.gpsimd.tensor_tensor(a, a, v, ALU.mult))
    link(nc.gpsimd.tensor_tensor(a, a, minus_half, ALU.mult))
    link(nc.gpsimd.tensor_tensor(a, a, three_halves, ALU.add))
    link(nc.gpsimd.tensor_tensor(r, y, a, ALU.mult))
    link(nc.gpsimd.tensor_tensor(a, stats[:, 0:1], r, ALU.mult))
    return nc.gpsimd.tensor_tensor(nb, a, minus_one, ALU.mult)


NORM_LINKS = 8
NORM_CONSTS = (-0.5, EPS, 1.5, -1.0)
CONSTS_READY = 6


def attention(nc, ident, consts, consts_ready, x_tok, ctx_kv, Wq, bq, Wk, bk, Wv, bv, x2_dram, shared,
              NT, NB, Q, D, DC, KC, DB, CPB, DH, H, NW, GROUP, G):
    SCALE = float(DH) ** -0.5
    DS = DH // NS
    K0 = KC * P
    WRING = 4
    XN2_PAIR = 5
    PROJECT_AT = 11
    PV_ORDER = tuple(range(1, DB)) + (0,)
    EXP_AFTER = (1, 2, 4, 6)
    W_EARLY, W_HALF, W_MORE = 2, 6, 8
    with ExitStack() as ctx:
        def sb(name, shape, dt=F32):
            return ctx.enter_context(nc.sbuf_tensor(name, shape, dt))

        def psum(name, shape):
            return ctx.enter_context(nc.psum_tensor(name, shape, F32))

        def sem(name):
            return ctx.enter_context(nc.semaphore(name))

        xa, xb, xn1T, last, prod = shared.xa, shared.xb, shared.xn1T, shared.last, shared.prod
        qkv, top, den, num, rden, o = shared.qkv, shared.top, shared.den, shared.num, shared.rden, shared.o

        keys = sb("keys", [P, DB + 1, NB, KC, 512])
        xn = sb("xn", [P, D])
        xn2T = sb("xn2T", [P, DC, P])
        keysT = shared.keysT.rearrange("p (r b k) -> p r b k", b=NB, k=K0)
        wqkv = sb("wqkv", [P, DC, NW])
        bias_qkv = sb("bias_qkv", [P, NW])
        wstage = ([prod[:, 2 * h:2 * h + 2].rearrange("p s q k -> p (s q k)") for h in range(2)]
                  + [keys[:, 0, 2 * h:2 * h + 2].rearrange("p b c n -> p (b c n)") for h in range(2)])
        junk = sb("junk", [P, D], BF16)
        probs = sb("probs", [P, K0])
        probsT = sb("probsT", [P, KC, P])
        bn1 = sb("bn1", [P, DB, 6])
        bn2 = sb("bn2", [P, DB, 6])
        mv1 = sb("mv1", [P, 2])
        mv2 = sb("mv2", [P, 2])
        nf1 = sb("nf1", [P, 5])
        nf2 = sb("nf2", [P, 5])
        s_last = sb("s_last", [P, 2])
        row = sb("row", [P, 8])
        kext = sb("kext", [P, 2])
        qlow = sb("qlow", [P, DH])

        bank = [psum(f"bank{n}", [P, 512]) for n in range(4)]
        scores = psum("scores", [P, 512])
        pvb = [psum(f"pv{n}", [P, 512]) for n in range(2)]
        qkv_sums = psum("qkv_sums", [P, 512])

        x_loaded = [sem(f"x_loaded{n}") for n in range(2)]
        last_loaded = [sem(f"last_loaded{n}") for n in range(2)]
        keys_loaded = [sem(f"keys_loaded{n}") for n in range(DB + 1)]
        w_loaded = [sem(f"w_loaded{n}") for n in range(WRING)]
        small_loaded = sem("small_loaded")
        wkv_loaded = sem("wkv_loaded")
        w_summed = sem("w_summed")
        bank_full = [sem(f"bank_full{n}") for n in range(4)]
        bank_emptied = [sem(f"bank_emptied{n}") for n in range(4)]
        chunk_scored = sem("chunk_scored")
        qkv_done = sem("qkv_done")
        qkv_read = sem("qkv_read")
        probsT_done = sem("probsT_done")
        probsT_read = sem("probsT_read")
        pv_filled = sem("pv_filled")
        pv_emptied = sem("pv_emptied")
        stats1_ready = sem("stats1_ready")
        stats2_ready = sem("stats2_ready")
        factors1_ready = sem("factors1_ready")
        factors2_ready = sem("factors2_ready")
        xn1_ready = sem("xn1_ready")
        xn2_ready = sem("xn2_ready")
        last_scored = sem("last_scored")
        negmax_ready = sem("negmax_ready")
        probs_ready = sem("probs_ready")
        residual_ready = sem("residual_ready")
        top_ready = sem("top_ready")
        prod_ready = sem("prod_ready")
        exp_ready = sem("exp_ready")
        den_ready = sem("den_ready")
        weighted_ready = sem("weighted_ready")
        num_ready = sem("num_ready")
        o_ready = sem("o_ready")
        x2_ready = sem("x2_ready")
        x2_stored = [sem(f"x2_stored{n}") for n in range(2)]
        softmax_step = sem("softmax_step")
        dve_passed = sem("dve_passed")
        sp_passed = sem("sp_passed")
        top_step = sem("top_step")
        ext_step = sem("ext_step")
        bn1_step = sem("bn1_step")
        bn2_step = sem("bn2_step")
        rden_step = sem("rden_step")
        bias_step = sem("bias_step")
        outer_step = sem("outer_step")
        norm1_step = sem("norm1_step")
        norm2_step = sem("norm2_step")

        def xn1_use(i):
            return 1 if isinstance(i, int) and i == 0 else i * 10

        def pair_use(i, j):
            if isinstance(i, int) and i == 0:
                return j + 2
            return i * 10 + (j + 1 if j < XN2_PAIR else j + 2)

        def xn2_use(i):
            return i * 10 + (XN2_PAIR + 1) if not isinstance(i, int) or i < NT else i * 10

        def tiles(eng, tile):
            tile(0, 0)
            tile(1, 1)
            with eng.Fori(1, NT // 2 - 1) as j:
                tile(j * 2, 0)
                tile(j * 2 + 1, 1)
            tile(NT - 2, 0)
            tile(NT - 1, 1)

        def landed(i, p):
            return i * 8 + (16 - 8 * p)

        def slot(d, p):
            return DB if d == 0 and p == 1 else d

        def keys_landed(i, p, d):
            return landed(i, p) * NB if d == 0 else (i + 1) * (16 * NB)

        block = ctx.enter_context(nc.Block())

        @block.sync
        def _(sp):
            def load_x(i, p, freed=0):
                row0 = at(sp, i * P)
                wait(sp, residual_ready, freed)
                sp.dma_start(xa[:, p, :], x_tok[bass.ds(row0, P), :]).then_inc(x_loaded[p], 16)

            def load_last(i, p):
                batch = [at(sp, i * NB + b) for b in range(NB)]
                wait(sp, residual_ready, i - 1)
                for b in range(NB):
                    sp.dma_start(last[b * Q:(b + 1) * Q, p, :],
                                 ctx_kv[bass.ds(batch[b], 1), K0, :].broadcast_to((Q, D))
                                 ).then_inc(last_loaded[p], 16)

            def load_block(i, p, d, batch):
                for b in range(NB):
                    sp.dma_start(keys[:, slot(d, p), b],
                                 ctx_kv[bass.ds(batch[b], 1), 0:K0, d * 512:(d + 1) * 512]
                                 .rearrange("a (c p) n -> p (a c) n", p=P)
                                 ).then_inc(keys_loaded[slot(d, p)], 16)

            def load_first(i, p):
                batch = [at(sp, i * NB + b) for b in range(NB)]
                wait(sp, pv_filled, i * DB - DB)
                pass_by(sp, sp_passed)
                load_block(i, p, 0, batch)

            def load_others(i, p):
                batch = [at(sp, i * NB + b) for b in range(NB)]
                for n, d in enumerate(PV_ORDER[:-1]):
                    wait(sp, pv_filled, i * DB + (n + 1 - DB))
                    pass_by(sp, sp_passed)
                    load_block(i, p, d, batch)

            def store_x2(m, p):
                row0 = at(sp, m * P)
                wait(sp, x2_ready, m + 1)
                sp.dma_start(x2_dram[bass.ds(row0, P), :], xb[:, p, :]).then_inc(x2_stored[p], 16)

            load_x(0, 0)
            load_first(0, 0)
            load_others(0, 0)
            load_last(0, 0)
            load_x(1, 1)
            load_last(1, 1)
            load_first(1, 1)

            def tile(i, p):
                if late(i, 2):
                    store_x2(i - 2, p)
                if not isinstance(i, int) or i + 1 < NT:
                    load_others(i + 1, 1 - p)
                if not isinstance(i, int) or i + 2 < NT:
                    load_x(i + 2, p, freed=i + 1)
                    load_last(i + 2, p)
                    if isinstance(i, int) and i == 0:
                        sp.wait_ge(w_summed, DC)
                    load_first(i + 2, p)

            tiles(sp, tile)
            sp.wait_ge(residual_ready, NT - 1)
            sp.dma_start(shared.rng, shared.ranges).then_inc(shared.rng_loaded, 16)
            sp.dma_start(last[:, 0, :].bitcast(I32), shared.q_rows[0]).then_inc(shared.rows_loaded[0], 16)
            sp.wait_ge(residual_ready, NT)
            sp.dma_start(last[:, 1, :].bitcast(I32), shared.q_rows[1]).then_inc(shared.rows_loaded[1], 16)
            sp.wait_ge(chunk_scored, NT * DC)
            for t in (2, 3):
                sp.dma_start(shared.row_slots[t].bitcast(I32), shared.q_rows[t]).then_inc(shared.rows_loaded[t], 16)
            for p in range(2):
                sp.wait_ge(x2_stored[p], 16 * (NT // 2 - 1))

        @block.tensor
        def _(pe):
            def turn(n, s, blocks):
                wait(pe, bank_emptied[s], n - 1)
                for j, block_in in enumerate(blocks):
                    mm = nc.tensor.transpose(bank[s][:, j * P:(j + 1) * P], block_in, ident[:])
                mm.then_inc(bank_full[s], 1)

            def turn_tokens(n, source):
                for u in range(4):
                    turn(n, u, [source[:, (4 * u + j) * P:(4 * u + j + 1) * P] for j in range(4)])

            def turn_chunk(i, p, c):
                block_slot = slot(c // CPB, p)
                if c % CPB == 0:
                    pe.wait_ge(keys_loaded[block_slot], keys_landed(i, p, c // CPB))
                for h in range(2):
                    turn(pair_use(i, c // 2), 2 * (c % 2) + h,
                         [keys[:, block_slot, 2 * h + b, kc, (c % CPB) * P:(c % CPB + 1) * P]
                          for b in range(2) for kc in range(KC)])

            def score_chunk(i, c):
                if c == 0:
                    wait(pe, probsT_read, i)
                if c % 4 == 0:
                    pe.wait_ge(bank_emptied[c // 4], xn1_use(i))
                for h in range(2):
                    pe.wait_ge(bank_emptied[2 * (c % 2) + h], pair_use(i, c // 2))
                for b in range(NB):
                    mm = nc.tensor.matmul(scores[b * Q:(b + 1) * Q, 0:K0], xn1T[:, c, b * Q:(b + 1) * Q],
                                          keysT[:, c % 4, b, :], start=(c == 0), stop=(c == DC - 1))
                mm.then_inc(chunk_scored, 1)

            def project(i):
                wait(pe, qkv_read, i - 1)
                for u in range(4):
                    pe.wait_ge(bank_emptied[u], xn2_use(i))
                for c in range(DC):
                    mm = nc.tensor.matmul(qkv_sums[:, 0:NW], xn2T[:, c, :], wqkv[:, c, :],
                                          start=(c == 0), stop=(c == DC - 1))
                mm.then_inc(qkv_done, 1)

            def turn_xn1(i):
                pe.wait_ge(xn1_ready, i + 1)
                turn_tokens(xn1_use(i), xn)

            def turn_ahead(i, p):
                turn_xn1(i)
                turn_chunk(i, p, 0)
                turn_chunk(i, p, 1)

            def tile(i, p):
                for c in range(DC):
                    if c + 2 < DC:
                        turn_chunk(i, p, c + 2)
                    if c + 2 == 2 * XN2_PAIR - 1 and late(i, 1):
                        pe.wait_ge(xn2_ready, i)
                        turn_tokens(xn2_use(i), xn)
                    if c == PROJECT_AT and late(i, 2):
                        project(i)
                    score_chunk(i, c)
                second = isinstance(i, int) and i == 1
                if second:
                    turn_xn1(2)
                elif not isinstance(i, int) or i + 1 < NT:
                    turn_ahead(i + 1, 1 - p)
                pe.wait_ge(probs_ready, (i + 1) * 2)
                for kc in range(KC):
                    mm = nc.tensor.transpose(scores[:, kc * P:(kc + 1) * P], probs[:, kc * P:(kc + 1) * P],
                                             ident[:])
                mm.then_inc(probsT_done, 1)
                pe.wait_ge(probsT_read, i + 1)
                for n, d in enumerate(PV_ORDER):
                    wait(pe, pv_emptied, i * DB + (n - 1))
                    for kc in range(KC):
                        for b in range(NB):
                            mm = nc.tensor.matmul(pvb[n % 2][b * Q:(b + 1) * Q, :],
                                                  probsT[:, kc, b * Q:(b + 1) * Q],
                                                  keys[:, slot(d, p), b, kc, :],
                                                  start=(kc == 0), stop=(kc == KC - 1))
                    mm.then_inc(pv_filled, 1)
                if second:
                    pe.wait_ge(w_summed, DC)
                    pe.wait_ge(wkv_loaded, 32)
                    project(1)
                    turn_chunk(2, 0, 0)
                    turn_chunk(2, 0, 1)

            pe.wait_ge(consts_ready, CONSTS_READY)
            turn_ahead(0, 0)
            tiles(pe, tile)
            pe.wait_ge(xn2_ready, NT)
            turn_tokens(xn2_use(NT), xn)
            project(NT)

        @block.scalar
        def _(act):
            def empty(n, s, target):
                act.wait_ge(bank_full[s], n)
                nc.scalar.copy(target, bank[s][:]).then_inc(bank_emptied[s], 1)

            def empty_tokens(n, target):
                for u in range(4):
                    empty(n, u, target[:, 4 * u:4 * u + 4, :].rearrange("p c n -> p (c n)"))

            def exp_slice(m, s):
                act.wait_ge(prod_ready, m * NS + (s + 1))
                nc.scalar.activation(prod[:, s], prod[:, s], ACT.Exp, scale=SCALE).then_inc(exp_ready, 1)

            def empty_chunk(i, c):
                wait(act, chunk_scored, i * DC + (c - 3))
                for h in range(2):
                    empty(pair_use(i, c // 2), 2 * (c % 2) + h,
                          keysT[:, c % 4, 2 * h:2 * h + 2, :].rearrange("p b k -> p (b k)"))

            def tile(i, p):
                for c in range(DC):
                    if c >= 2:
                        empty_chunk(i, c)
                    if c == 2 * XN2_PAIR - 1 and late(i, 1):
                        empty_tokens(xn2_use(i), xn2T)
                    if c in EXP_AFTER and late(i, 2):
                        exp_slice(i - 2, EXP_AFTER.index(c))
                if not isinstance(i, int) or i + 1 < NT:
                    empty_tokens(xn1_use(i + 1), xn1T)
                act.wait_ge(negmax_ready, i + 1)
                wait(act, probsT_done, i)
                nc.scalar.activation(probs[:], scores[:, 0:K0], ACT.Exp, bias=row[:, 1:2],
                                     accum_out=row[:, 2:3]).then_inc(probs_ready, 1)
                nc.scalar.activation(row[:, 3:4], s_last[:, p:p + 1], ACT.Exp,
                                     bias=row[:, 1:2]).then_inc(probs_ready, 1)
                act.wait_ge(probsT_done, i + 1)
                nc.scalar.copy(probsT[:].rearrange("p c n -> p (c n)"), scores[:, 0:K0]).then_inc(probsT_read, 1)
                if not isinstance(i, int) or i + 1 < NT:
                    empty_chunk(i + 1, 0)
                    empty_chunk(i + 1, 1)

            empty_tokens(xn1_use(0), xn1T)
            empty_chunk(0, 0)
            empty_chunk(0, 1)
            tiles(act, tile)
            for s in range(NS):
                exp_slice(NT - 2, s)
            empty_tokens(xn2_use(NT), xn2T)

        @block.vector
        def _(dve):
            def stats1(i, p):
                dve.wait_ge(x_loaded[p], landed(i, p))
                wait(dve, factors1_ready, i)
                for d in range(DB):
                    nc.vector.bn_stats(bn1[:, d], xa[:, p, d * 512:(d + 1) * 512]).then_inc(bn1_step, 1)
                dve.wait_ge(bn1_step, (i + 1) * DB)
                pass_by(dve, dve_passed)
                nc.vector.bn_aggr(mv1[:], bn1[:].rearrange("p d s -> p (d s)")).then_inc(stats1_ready, 1)

            def normalise(i, factors_ready, xn_ready, target, source, factors):
                dve.wait_ge(factors_ready, i + 1)
                nc.vector.tensor_scalar(target, source, factors[:, 3:4], factors[:, 4:5], ALU.mult,
                                        ALU.add).then_inc(xn_ready, 1)

            def qkv_out(i, p):
                q, k = qkv[:, p, 0:DH], qkv[:, p, DH:2 * DH]
                dve.wait_ge(qkv_done, i)
                nc.vector.tensor_tensor(qkv[:, p], qkv_sums[:, 0:NW], bias_qkv[:], ALU.add).then_inc(qkv_read, 1)
                dve.wait_ge(qkv_read, i)
                nc.vector.tensor_reduce(kext[:, 0:1], k, AX.X, ALU.max).then_inc(ext_step, 1)
                nc.vector.tensor_reduce(kext[:, 1:2], k, AX.X, ALU.min).then_inc(ext_step, 1)
                dve.wait_ge(ext_step, i * 2)
                nc.vector.tensor_scalar(qlow[:], q, kext[:, 1:2], None, ALU.mult).then_inc(top_step, 1)
                dve.wait_ge(top_step, i)
                nc.vector.scalar_tensor_tensor(top[:, p], q, kext[:, 0:1], qlow[:],
                                               ALU.mult, ALU.max).then_inc(top_ready, 1)

            def sum_probs(m, s):
                dve.wait_ge(exp_ready, m * NS + (s + 1))
                nc.vector.tensor_reduce(den[:, s * DS:(s + 1) * DS], prod[:, s], AX.X,
                                        ALU.add).then_inc(den_ready, 1)

            def sum_weighted(m, s):
                dve.wait_ge(weighted_ready, m * NS + (s + 1))
                nc.vector.tensor_reduce(num[:, s * DS:(s + 1) * DS], prod[:, s], AX.X,
                                        ALU.add).then_inc(num_ready, 1)

            def finish_self(m):
                dve.wait_ge(den_ready, m * NS + NS)
                nc.vector.reciprocal(rden[:], den[:]).then_inc(rden_step, 1)
                dve.wait_ge(rden_step, m + 1)
                dve.wait_ge(num_ready, m * NS + NS)
                nc.vector.tensor_tensor(o[:], num[:], rden[:], ALU.mult).then_inc(o_ready, 1)

            def sum_heads(c):
                dve.wait_ge(w_loaded[c % WRING], 16 * (c // WRING + 1))
                nc.vector.tensor_reduce(wqkv[:, c, 0:DH],
                                        wstage[c % WRING].rearrange("p (d h) -> p d h", h=H),
                                        AX.X, ALU.add).then_inc(w_summed, 1)

            def score_last(i, p):
                dve.wait_ge(last_loaded[p], i * (8 * NB) + (16 - 8 * p) * NB)
                dve.wait_ge(xn1_ready, i + 1)
                nc.vector.tensor_tensor_reduce(out=junk[:], in0=xn[:], in1=last[:, p, :], scale=1.0,
                                               scalar=0.0, op0=ALU.mult, op1=ALU.add,
                                               accum_out=s_last[:, p:p + 1]).then_inc(last_scored, 1)

            def tile(i, p):
                link = chain(dve, softmax_step, i * 4)
                more = not isinstance(i, int) or i + 1 < NT
                if isinstance(i, int) and i == 1:
                    for c in range(W_EARLY):
                        sum_heads(c)
                if late(i, 2):
                    sum_probs(i - 2, 0)
                    sum_probs(i - 2, 1)
                    sum_weighted(i - 2, 0)
                    sum_probs(i - 2, 2)
                    sum_weighted(i - 2, 1)
                    sum_probs(i - 2, 3)
                    sum_weighted(i - 2, 2)
                    sum_weighted(i - 2, 3)
                    finish_self(i - 2)
                if more:
                    stats1(i + 1, 1 - p)
                if late(i, 2):
                    qkv_out(i, 1 - p)
                if more:
                    dve.wait_ge(bank_full[3], xn2_use(i) if late(i, 1) else xn1_use(i))
                    dve.wait_ge(last_scored, i + 1)
                    normalise(i + 1, factors1_ready, xn1_ready, xn[:], xa[:, 1 - p, :], nf1)
                    if late(i, 1):
                        score_last(i + 1, 1 - p)
                if isinstance(i, int) and i == 1:
                    for c in range(W_EARLY, W_HALF):
                        sum_heads(c)
                dve.wait_ge(chunk_scored, (i + 1) * DC)
                wait(dve, probs_ready, i * 2)
                link(nc.vector.tensor_reduce(row[:, 0:1], scores[:, 0:K0], AX.X, ALU.max))
                dve.wait_ge(last_scored, i + 1)
                nc.vector.tensor_scalar(row[:, 1:2], row[:, 0:1], s_last[:, p:p + 1], -1.0, ALU.max,
                                        ALU.mult).then_inc(negmax_ready, 1)
                dve.wait_ge(probs_ready, (i + 1) * 2)
                link(nc.vector.tensor_tensor(row[:, 4:5], row[:, 2:3], row[:, 3:4], ALU.add))
                link(nc.vector.reciprocal(row[:, 5:6], row[:, 4:5]))
                link(nc.vector.tensor_tensor(row[:, 6:7], row[:, 3:4], row[:, 5:6], ALU.mult))
                if late(i, 2):
                    dve.wait_ge(x2_stored[p], landed(i - 2, p))
                nc.vector.scalar_tensor_tensor(xb[:, p, :], last[:, p, :], row[:, 6:7], xa[:, p, :], ALU.mult,
                                               ALU.add).then_inc(residual_ready, 1)
                if isinstance(i, int) and i == 1:
                    for c in range(W_HALF, W_MORE):
                        sum_heads(c)
                dve.wait_ge(residual_ready, i + 1)
                wait(dve, factors2_ready, i)
                for n, d in enumerate(PV_ORDER):
                    part = xb[:, p, d * 512:(d + 1) * 512]
                    dve.wait_ge(pv_filled, i * DB + (n + 1))
                    nc.vector.scalar_tensor_tensor(part, pvb[n % 2][:], row[:, 5:6], part, ALU.mult,
                                                   ALU.add).then_inc(pv_emptied, 1)
                    dve.wait_ge(pv_emptied, i * DB + (n + 1))
                    nc.vector.bn_stats(bn2[:, d], part).then_inc(bn2_step, 1)
                dve.wait_ge(bn2_step, (i + 1) * DB)
                pass_by(dve, dve_passed)
                nc.vector.bn_aggr(mv2[:], bn2[:].rearrange("p d s -> p (d s)")).then_inc(stats2_ready, 1)
                if isinstance(i, int) and i == 1:
                    for c in range(W_MORE, DC):
                        sum_heads(c)
                if isinstance(i, int) and i == NT - 1:
                    dve.wait_ge(shared.rng_loaded, 16)
                    nc.vector.tensor_tensor(shared.step_of, shared.rng[:, :, :, 1], shared.rng[:, :, :, 0],
                                            ALU.subtract).then_inc(shared.range_step, 1)
                    nc.vector.tensor_scalar(shared.least_of, shared.rng[:, :, :, 0], LO, None,
                                            ALU.mult).then_inc(shared.ranges_ready, 1)
                    dve.wait_ge(shared.range_step, 1)
                    nc.vector.tensor_scalar(shared.step_of, shared.step_of, LO / LEVELS, None,
                                            ALU.mult).then_inc(shared.ranges_ready, 1)
                if more:
                    dve.wait_ge(bank_full[3], xn1_use(i + 1))
                if isinstance(i, int) and i == 0:
                    score_last(1, 1)
                dve.wait_ge(last_scored, i + 2 if more else NT)
                normalise(i, factors2_ready, xn2_ready, xn[:], xb[:, p, :], nf2)
                if isinstance(i, int) and i == 1:
                    qkv_out(i, 0)

            stats1(0, 0)
            normalise(0, factors1_ready, xn1_ready, xn[:], xa[:, 0, :], nf1)
            score_last(0, 0)
            dve.wait_ge(small_loaded, 48)
            nc.vector.tensor_reduce(bias_qkv[:, 0:DH], xb[:, 0, :].rearrange("p (d h) -> p d h", h=H), AX.X,
                                    ALU.add).then_inc(bias_step, 1)
            dve.wait_ge(bias_step, 1)
            tiles(dve, tile)
            dve.wait_ge(shared.ranges_ready, 2)
            scale_rows(nc, dve, shared, 0, GROUP, G)
            for s in range(NS):
                sum_probs(NT - 2, s)
            scale_rows(nc, dve, shared, 1, GROUP, G)
            qkv_out(NT, 1)

        @block.gpsimd
        def _(pool):
            def factors(i, step, mv, nf, stats_ready, factors_ready, xn_ready):
                link = chain(pool, step, i * NORM_LINKS)
                pool.wait_ge(stats_ready, i + 1)
                wait(pool, xn_ready, i)
                norm_factors(nc, pool, link, mv, nf, consts).then_inc(factors_ready, 1)

            def product(m, p, s):
                n = m * NS + (s + 1)
                S = prod[:, s]
                nc.gpsimd.tensor_tensor(S, qkv[:, p, s * DS:(s + 1) * DS].unsqueeze(2).broadcast_to((P, DS, DH)),
                                        qkv[:, p, DH:2 * DH].unsqueeze(1).broadcast_to((P, DS, DH)),
                                        ALU.mult).then_inc(outer_step, 1)
                pool.wait_ge(outer_step, n)
                nc.gpsimd.tensor_tensor(S, S, top[:, p, s * DS:(s + 1) * DS].unsqueeze(2)
                                        .broadcast_to((P, DS, DH)), ALU.subtract).then_inc(prod_ready, 1)

            def weigh(m, p, s):
                pool.wait_ge(den_ready, m * NS + (s + 1))
                S = prod[:, s]
                nc.gpsimd.tensor_tensor(S, S, qkv[:, p, 2 * DH:3 * DH].unsqueeze(1).broadcast_to((P, DS, DH)),
                                        ALU.mult).then_inc(weighted_ready, 1)

            def products(m, p, slices):
                pool.wait_ge(top_ready, m + 1)
                for s in slices:
                    product(m, p, s)

            def add_self(m, p):
                pool.wait_ge(o_ready, m + 1)
                rows = xb[:, p, :].rearrange("p (d h) -> p d h", h=H)
                nc.gpsimd.tensor_tensor(rows, rows,
                                        o[:].unsqueeze(2).broadcast_to((P, DH, H)),
                                        ALU.add).then_inc(x2_ready, 1)

            def tile(i, p):
                for s in range(NS):
                    weigh(i - 2, p, s)
                add_self(i - 2, p)
                if not isinstance(i, int) or i + 1 < NT:
                    factors(i + 1, norm1_step, mv1, nf1, stats1_ready, factors1_ready, xn1_ready)
                products(i - 1, 1 - p, range(NS))
                factors(i, norm2_step, mv2, nf2, stats2_ready, factors2_ready, xn2_ready)

            nc.gpsimd.memset(ident[:], 0.0).then_inc(consts_ready, 1)
            for n, value in enumerate(NORM_CONSTS):
                nc.gpsimd.memset(consts[:, n:n + 1], value).then_inc(consts_ready, 1)
            pool.wait_ge(consts_ready, CONSTS_READY - 1)
            nc.gpsimd.affine_select(out=ident[:], in_=ident[:], compare_op=ALU.not_equal, fill=1.0, base=0,
                                    pattern=[[-1, P]], channel_multiplier=1).then_inc(consts_ready, 1)
            pool.dma_start(xb[:, 0, :], bq.rearrange("d h -> (d h)").unsqueeze(0).broadcast_to((P, DH * H))
                           ).then_inc(small_loaded, 16)
            pool.dma_start(bias_qkv[:, DH:2 * DH], bk.rearrange("d o -> o d").broadcast_to((P, DH))
                           ).then_inc(small_loaded, 16)
            pool.dma_start(bias_qkv[:, 2 * DH:3 * DH], bv.rearrange("d o -> o d").broadcast_to((P, DH))
                           ).then_inc(small_loaded, 16)

            def load_w(c):
                wait(pool, w_summed, c - WRING + 1)
                if c == 2:
                    pool.wait_ge(pv_filled, DB)
                pool.dma_start(wstage[c % WRING], Wq[c * P:(c + 1) * P].rearrange("p d h -> p (d h)")
                               ).then_inc(w_loaded[c % WRING], 16)

            factors(0, norm1_step, mv1, nf1, stats1_ready, factors1_ready, xn1_ready)
            factors(1, norm1_step, mv1, nf1, stats1_ready, factors1_ready, xn1_ready)
            pool.dma_start(wqkv[:, :, DH:2 * DH], Wk.rearrange("(c p) d o -> p c (d o)", p=P)
                           ).then_inc(wkv_loaded, 16)
            pool.dma_start(wqkv[:, :, 2 * DH:3 * DH], Wv.rearrange("(c p) d o -> p c (d o)", p=P)
                           ).then_inc(wkv_loaded, 16)
            for c in range(2):
                load_w(c)
            factors(0, norm2_step, mv2, nf2, stats2_ready, factors2_ready, xn2_ready)
            for c in range(2, W_HALF):
                load_w(c)
            factors(2, norm1_step, mv1, nf1, stats1_ready, factors1_ready, xn1_ready)
            for c in range(W_HALF, DC):
                load_w(c)
            factors(1, norm2_step, mv2, nf2, stats2_ready, factors2_ready, xn2_ready)
            products(0, 0, range(NS))
            with pool.Fori(1, NT // 2 - 1) as j:
                tile(j * 2, 0)
                tile(j * 2 + 1, 1)
            tile(NT - 2, 0)
            tile(NT - 1, 1)
            add_least(nc, pool, shared, 0, GROUP, G)
            for s in range(NS):
                weigh(NT - 2, 0, s)


def feed_forward(nc, ident, consts, x2_dram, bias, out_tok, shared, NT, D, DC, DB, CPB, DH, H, GROUP, G):
    SCALE = float(DH) ** -0.5
    DS = DH // NS
    SELF_ADDS = (5, 11)
    SELF_PRODUCTS = (5, 6, 7, 8)
    SELF_EXPS = (5, 6, 7, 8)
    SELF_SUMS = {5: (0,), 6: (1,), 7: (2,), 8: (3,), 10: (4, 5), 11: (6, 7)}
    SELF_WEIGHS = {9: (0, 1), 10: (2, 3)}
    SELF_FINISH = 11
    SELF_STORES = (7, 12)
    OT = D // P
    with ExitStack() as ctx:
        def sb(name, shape, dt=F32):
            return ctx.enter_context(nc.sbuf_tensor(name, shape, dt))

        def sem(name):
            return ctx.enter_context(nc.semaphore(name))

        w_high = [sb(f"w_high{d}", [P, DC, 512], F16)[:] for d in range(2)] + [shared.w_high_2, shared.w_high_last]
        w_low = [sb(f"w_low{d}", [P, DC, 512], F16)[:] for d in range(DB - 1)] + [shared.w_low_last]
        bias_row = sb("bias_row", [P, D], F16)
        xn3 = sb("xn3", [P, D])
        row_slots = shared.row_slots

        def x2(i, p):
            return shared.x2[:, p, :] if isinstance(i, int) and i < 2 else shared.last[:, p, :]

        xb, qkv, top, prod = shared.xb, shared.qkv, shared.top, shared.prod
        den, num, rden, o = shared.den, shared.num, shared.rden, shared.o
        x_high = sb("x_high", [P, 2, DC, P], F16)
        x_low = sb("x_low", [P, 2, DC, P], F16)
        x_small = sb("x_small", [P, 2, DC, P], F16)
        bn3 = sb("bn3", [P, DB, 6])
        mv3 = sb("mv3", [P, 2])
        nf3 = sb("nf3", [P, 5])
        bank = [ctx.enter_context(nc.psum_tensor(f"turned{n}", [P, 512], F32)) for n in range(4)]
        y = [ctx.enter_context(nc.psum_tensor(f"y{n}", [P, 512], F32)) for n in range(DB)]

        bias_loaded = sem("bias_loaded")
        x2_loaded = [sem(f"x2_loaded{n}") for n in range(2)]
        out_stored = [sem(f"out_stored{n}") for n in range(2)]
        turned_full = [sem(f"turned_full{n}") for n in range(4)]
        high_ready = sem("high_ready")
        turned_emptied = [sem(f"turned_emptied{n}") for n in range(4)]
        small_ready = sem("small_ready")
        bn3_step = sem("bn3_step")
        dve_passed3 = sem("dve_passed3")
        stats3_ready = sem("stats3_ready")
        norm3_step = sem("norm3_step")
        factors3_ready = sem("factors3_ready")
        xn3_ready = sem("xn3_ready")
        biased = sem("biased")
        before_totals = sem("before_totals")
        before_rden = sem("before_rden")
        before_ready = sem("before_ready")
        self_step = sem("self_step")
        self_products = sem("self_products")
        self_exps = sem("self_exps")
        self_summed = sem("self_summed")
        self_weighted = sem("self_weighted")
        self_totals = sem("self_totals")
        self_rden = sem("self_rden")
        self_ready = sem("self_ready")
        self_added = sem("self_added")
        self_stored = sem("self_stored")
        y_filled = sem("y_filled")
        y_emptied = sem("y_emptied")

        TPB = CPB

        def tiles(eng, tile):
            with eng.Fori(1, NT // 2 - 1) as j:
                tile(j * 2, 0)
                tile(j * 2 + 1, 1)
            tile(NT - 2, 0)
            tile(NT - 1, 1)

        def more(i):
            return not isinstance(i, int) or i + 1 < NT

        def landed(i, p):
            return i * 8 + (16 - 8 * p)

        def rows_use(t):
            return t + 1 if t < TPB else t + 3

        def rows_beside(d, p):
            t = TPB * (d + 1) + 2 * p
            if d == DB - 1:
                return (), ()
            if d == 0:
                return ((t - 1,), (t, t + 1)) if p == 1 else ((), (t,))
            return (t,), (t + 1,)

        def token_use(i):
            return TPB + 1 + i if isinstance(i, int) and i < 2 else i + (OT + 1)

        block = ctx.enter_context(nc.Block())

        @block.sync
        def _(sp):
            def load_x2(i, p, freed=None):
                row0 = at(sp, i * P)
                if freed is not None:
                    sp.wait_ge(*freed)
                sp.dma_start(x2(i, p), x2_dram[bass.ds(row0, P), :]).then_inc(x2_loaded[p], 16)

            def store(i, p, count):
                row0 = at(sp, i * P)
                sp.wait_ge(y_emptied, count)
                sp.dma_start(out_tok[bass.ds(row0, P), :], x2(i, p)).then_inc(out_stored[p], 16)

            def load_rows(t):
                sp.wait_ge(turned_full[3], rows_use(t - (4 if t < EARLY_ROWS + 2 else 2)))
                sp.dma_start(row_slots[row_slot(t)].bitcast(I32), shared.q_rows[t]
                             ).then_inc(shared.rows_loaded[row_slot(t)], 16)

            def store_self(m, p):
                sp.wait_ge(self_added, p + 1)
                sp.dma_start(x2_dram[m * P:(m + 1) * P, :], xb[:, p, :]).then_inc(self_stored, 16)

            load_x2(0, 0)
            load_x2(1, 1)
            sp.dma_start(bias_row[:], bias.unsqueeze(0).broadcast_to((P, D))).then_inc(bias_loaded, 16)
            for t in range(4, OT):
                load_rows(t)
                if t == SELF_STORES[0]:
                    store_self(NT - 2, 0)
                if t == SELF_STORES[1]:
                    store_self(NT - 1, 1)
            load_x2(2, 0, freed=(turned_full[3], rows_use(OT - 2)))
            store(0, 0, 2 * DB - 1)
            store(1, 1, 2 * DB)

            def tile(i, p):
                if more(i):
                    load_x2(i + 1, 1 - p, freed=(out_stored[1 - p], landed(i - 1, 1 - p)))
                store(i, p, (i + 1) * DB)

            tiles(sp, tile)
            for p in range(2):
                sp.wait_ge(out_stored[p], 16 * (NT // 2))

        @block.tensor
        def _(pe):
            def turn(n, s, blocks):
                wait(pe, turned_emptied[s], n - 1)
                for j, block_in in enumerate(blocks):
                    mm = nc.tensor.transpose(bank[s][:, j * P:(j + 1) * P], block_in, ident[:])
                mm.then_inc(turned_full[s], 1)

            def turn_tokens(i):
                pe.wait_ge(xn3_ready, i + 1)
                for u in range(4):
                    turn(token_use(i), u, [xn3[:, (4 * u + j) * P:(4 * u + j + 1) * P] for j in range(4)])

            def turn_rows(t):
                pe.wait_ge(shared.w_ready, t + 1)
                for u in range(4):
                    turn(rows_use(t), u, [row_slots[row_slot(t)][:, (4 * u + j) * P:(4 * u + j + 1) * P]
                                          for j in range(4)])

            def product(p, d, bank_of, filled, halfway=()):
                wait(pe, y_emptied, filled - (DB - 1))
                for c in range(DC):
                    if c == DC // 2:
                        for t in halfway:
                            turn_rows(t)
                    nc.tensor.matmul(y[bank_of][:], x_high[:, p, c, :], w_high[d][:, c, :],
                                     start=(c == 0), stop=False)
                    nc.tensor.matmul(y[bank_of][:], x_low[:, p, c, :], w_high[d][:, c, :],
                                     start=False, stop=False)
                    mm = nc.tensor.matmul(y[bank_of][:], x_small[:, p, c, :], w_low[d][:, c, :],
                                          start=False, stop=(c == DC - 1))
                mm.then_inc(y_filled, 1)

            for t in range(TPB):
                turn_rows(t)
            turn_tokens(0)
            for d in range(DB):
                for u in range(4):
                    pe.wait_ge(turned_emptied[u], rows_use(TPB * (d + 1) - 1))
                for p in range(2):
                    pe.wait_ge(small_ready, p + 1)
                    product(p, d, (2 * d + p) % DB, 2 * d + p, halfway=rows_beside(d, p)[0])
                    if p == 0 and d in (0, DB - 1):
                        turn_tokens(1 if d == 0 else 2)
                    for t in rows_beside(d, p)[1]:
                        turn_rows(t)

            def tile(i, p):
                pe.wait_ge(small_ready, i + 1)
                for d in range(DB):
                    if d == 2 and more(i):
                        turn_tokens(i + 1)
                    product(p, d, d, i * DB + d)

            tiles(pe, tile)

        @block.scalar
        def _(act):
            def token_high(i, p):
                for u in range(4):
                    act.wait_ge(turned_full[u], token_use(i))
                    nc.scalar.copy(x_high[:, p, 4 * u:4 * u + 4, :].rearrange("p c n -> p (c n)"),
                                   bank[u][:]).then_inc(high_ready, 1)

            def rows_high(t):
                if t == OT - TPB:
                    act.wait_ge(self_totals, NS)
                for u in range(4):
                    act.wait_ge(turned_full[u], rows_use(t))
                    nc.scalar.activation(w_high[t // TPB][:, 4 * u:4 * u + 4, (t % TPB) * P:(t % TPB + 1) * P],
                                         bank[u][:].rearrange("p (c n) -> p c n", n=P), ACT.Copy,
                                         scale=1.0 / LO).then_inc(high_ready, 1)

            for t in range(TPB):
                rows_high(t)
            token_high(0, 0)
            token_high(1, 1)
            for t in range(TPB, OT):
                rows_high(t)
                if t in SELF_EXPS:
                    s = SELF_EXPS.index(t)
                    act.wait_ge(self_products, s + 1)
                    nc.scalar.activation(prod[:, s], prod[:, s], ACT.Exp, scale=SCALE).then_inc(self_exps, 1)
            token_high(2, 0)

            def tile(i, p):
                if more(i):
                    token_high(i + 1, 1 - p)

            tiles(act, tile)

        @block.vector
        def _(dve):
            def stats(i, p):
                dve.wait_ge(x2_loaded[p], landed(i, p))
                wait(dve, factors3_ready, i)
                for d in range(DB):
                    nc.vector.bn_stats(bn3[:, d], x2(i, p)[:, d * 512:(d + 1) * 512]).then_inc(bn3_step, 1)
                dve.wait_ge(bn3_step, (i + 1) * DB)
                pass_by(dve, dve_passed3)
                nc.vector.bn_aggr(mv3[:], bn3[:].rearrange("p d s -> p (d s)")).then_inc(stats3_ready, 1)

            def normalise(i, p):
                dve.wait_ge(factors3_ready, i + 1)
                if late(i, 1):
                    dve.wait_ge(turned_full[3], token_use(i - 1) if isinstance(i, int) else i + OT)
                nc.vector.tensor_scalar(xn3[:], x2(i, p), nf3[:, 3:4], nf3[:, 4:5], ALU.mult,
                                        ALU.add).then_inc(xn3_ready, 1)

            def token_low(i, p):
                for u in range(4):
                    dve.wait_ge(high_ready, 4 * (token_use(i) - 1) + u + 1 if isinstance(i, int)
                                else i * 4 + (4 * OT + u + 1))
                    part = slice(4 * u, 4 * u + 4)
                    nc.vector.tensor_tensor(x_low[:, p, part, :].rearrange("p c n -> p (c n)"), bank[u][:],
                                            x_high[:, p, part, :].rearrange("p c n -> p (c n)"),
                                            ALU.subtract).then_inc(turned_emptied[u], 1)
                nc.vector.tensor_scalar(x_small[:, p], x_high[:, p], 1.0 / LO, None,
                                        ALU.mult).then_inc(small_ready, 1)

            def rows_low(t):
                if t == OT - TPB:
                    dve.wait_ge(self_stored, 32)
                for u in range(4):
                    part = (slice(None), slice(4 * u, 4 * u + 4), slice((t % TPB) * P, (t % TPB + 1) * P))
                    dve.wait_ge(high_ready, 4 * (rows_use(t) - 1) + u + 1)
                    nc.vector.scalar_tensor_tensor(w_low[t // TPB][part], w_high[t // TPB][part], -LO,
                                                   bank[u][:].rearrange("p (c n) -> p c n", n=P),
                                                   ALU.mult, ALU.add).then_inc(turned_emptied[u], 1)

            def add_residual(i, p, d, bank_of, filled):
                dve.wait_ge(y_filled, filled)
                part = x2(i, p)[:, d * 512:(d + 1) * 512]
                nc.vector.tensor_tensor(part, y[bank_of][:], part, ALU.add).then_inc(y_emptied, 1)

            def sum_self(s):
                if s < NS:
                    dve.wait_ge(before_rden, 1)
                    dve.wait_ge(self_exps, s + 1)
                    nc.vector.tensor_reduce(den[:, s * DS:(s + 1) * DS], prod[:, s], AX.X,
                                            ALU.add).then_inc(self_summed, 1)
                else:
                    s -= NS
                    dve.wait_ge(before_ready, 1)
                    dve.wait_ge(self_weighted, s + 1)
                    nc.vector.tensor_reduce(num[:, s * DS:(s + 1) * DS], prod[:, s], AX.X,
                                            ALU.add).then_inc(self_totals, 1)

            def sum_weighted_before(s):
                nc.vector.tensor_reduce(num[:, s * DS:(s + 1) * DS], prod[:, s], AX.X,
                                        ALU.add).then_inc(before_totals, 1)

            def finish_before():
                nc.vector.reciprocal(rden[:], den[:]).then_inc(before_rden, 1)
                dve.wait_ge(before_rden, 1)
                dve.wait_ge(before_totals, NS)
                nc.vector.tensor_tensor(o[:], num[:], rden[:], ALU.mult).then_inc(before_ready, 1)

            def finish_self():
                dve.wait_ge(before_ready, 1)
                dve.wait_ge(self_summed, NS)
                nc.vector.reciprocal(rden[:], den[:]).then_inc(self_rden, 1)
                dve.wait_ge(self_rden, 1)
                dve.wait_ge(self_totals, NS)
                dve.wait_ge(self_added, 1)
                nc.vector.tensor_tensor(o[:], num[:], rden[:], ALU.mult).then_inc(self_ready, 1)

            scale_rows(nc, dve, shared, 2, GROUP, G)
            rows_low(0)
            scale_rows(nc, dve, shared, 3, GROUP, G)
            rows_low(1)
            stats(0, 0)
            rows_low(2)
            normalise(0, 0)
            rows_low(3)
            token_low(0, 0)
            scale_rows(nc, dve, shared, 4, GROUP, G)
            stats(1, 1)
            normalise(1, 1)
            scale_rows(nc, dve, shared, TPB + 1, GROUP, G)
            token_low(1, 1)
            for s in range(NS):
                sum_weighted_before(s)
            finish_before()
            for d in range(DB):
                for p in range(2):
                    for t in rows_beside(d, p)[0] + rows_beside(d, p)[1]:
                        if t > TPB and t + 1 < OT:
                            scale_rows(nc, dve, shared, t + 1, GROUP, G)
                        rows_low(t)
                        for s in SELF_SUMS.get(t, ()):
                            sum_self(s)
                        if t == SELF_FINISH:
                            finish_self()
                    if d == 0:
                        dve.wait_ge(biased, p + 1)
                    if d == DB - 1 and p == 0:
                        stats(2, 0)
                        normalise(2, 0)
                    if d == DB - 1 and p == 1:
                        token_low(2, 0)
                    add_residual(p, p, d, (2 * d + p) % DB, 2 * d + p + 1)
            def tile(i, p):
                if more(i):
                    stats(i + 1, 1 - p)
                    normalise(i + 1, 1 - p)
                dve.wait_ge(biased, i + 1)
                for d in range(DB):
                    if d == 2 and more(i):
                        token_low(i + 1, 1 - p)
                    add_residual(i, p, d, d, i * DB + (d + 1))

            tiles(dve, tile)

        @block.gpsimd
        def _(pool):
            def factors(i):
                link = chain(pool, norm3_step, i * NORM_LINKS)
                pool.wait_ge(stats3_ready, i + 1)
                wait(pool, xn3_ready, i)
                norm_factors(nc, pool, link, mv3, nf3, consts).then_inc(factors3_ready, 1)

            def add_bias(i, p):
                pool.wait_ge(xn3_ready, i + 1)
                nc.gpsimd.tensor_tensor(x2(i, p), x2(i, p), bias_row[:], ALU.add).then_inc(biased, 1)

            def add_self(p):
                rows = xb[:, p, :].rearrange("p (d h) -> p d h", h=H)
                nc.gpsimd.tensor_tensor(rows, rows, o[:].unsqueeze(2).broadcast_to((P, DH, H)),
                                        ALU.add).then_inc(self_added, 1)

            def product(s):
                S = prod[:, s]
                nc.gpsimd.tensor_tensor(S, qkv[:, 1, s * DS:(s + 1) * DS].unsqueeze(2).broadcast_to((P, DS, DH)),
                                        qkv[:, 1, DH:2 * DH].unsqueeze(1).broadcast_to((P, DS, DH)),
                                        ALU.mult).then_inc(self_step, 1)
                pool.wait_ge(self_step, s + 1)
                nc.gpsimd.tensor_tensor(S, S, top[:, 1, s * DS:(s + 1) * DS].unsqueeze(2)
                                        .broadcast_to((P, DS, DH)), ALU.subtract).then_inc(self_products, 1)

            def weigh(s):
                pool.wait_ge(self_summed, s + 1)
                S = prod[:, s]
                nc.gpsimd.tensor_tensor(S, S, qkv[:, 1, 2 * DH:3 * DH].unsqueeze(1).broadcast_to((P, DS, DH)),
                                        ALU.mult).then_inc(self_weighted, 1)

            add_least(nc, pool, shared, 1, GROUP, G)
            add_least(nc, pool, shared, 2, GROUP, G)
            add_least(nc, pool, shared, 3, GROUP, G)
            factors(0)
            for t in range(4, OT):
                add_least(nc, pool, shared, t, GROUP, G)
                if t == TPB:
                    factors(1)
                if t == TPB + 1:
                    pool.wait_ge(bias_loaded, 16)
                    add_bias(0, 0)
                    add_bias(1, 1)
                if t == SELF_ADDS[0]:
                    pool.wait_ge(before_ready, 1)
                    add_self(0)
                if t in SELF_PRODUCTS:
                    product(SELF_PRODUCTS.index(t))
                for s in SELF_WEIGHS.get(t, ()):
                    weigh(s)
                if t == SELF_ADDS[1]:
                    pool.wait_ge(self_ready, 1)
                    add_self(1)
            factors(2)
            add_bias(2, 0)

            def tile(i, p):
                if more(i):
                    factors(i + 1)
                    add_bias(i + 1, 1 - p)

            tiles(pool, tile)


_INS = ["x", "ctx_4096", "L0_attn_Wq", "L0_attn_bq", "L0_attn_Wk", "L0_attn_bk", "L0_attn_Wv", "L0_attn_bv",
        "L0_ffn_weight_q3", "L0_ffn_weight_ranges", "L0_ffn_bias"]


def kernel(**inputs):
    import numpy as np
    import concourse.bacc as bacc
    from concourse.bass_utils import run_bass_kernel_spmd

    nc = bacc.Bacc("TRN2", target_bir_lowering=False, num_devices=1)
    arrays, args = {}, []
    for name in _INS:
        a = np.ascontiguousarray(inputs[name])
        arrays[name] = a
        args.append(nc.dram_tensor(name, a.shape, mybir.dt.from_np(a.dtype), kind="ExternalInput").ap())
    shape = arrays["x"].shape
    out = nc.dram_tensor("out", shape, F32, kind="ExternalOutput").ap()
    build(nc, *args, out)
    return run_bass_kernel_spmd(nc, [arrays], core_ids=[0]).results[0]["out"]
```
